# Optimizing a Trainium2 kernel written in Bass

```python
import numpy as np
import jax
import jax.numpy as jnp

def _softmax(x, axis=-1):
    return jax.nn.softmax(x, axis=axis)

def _gelu(x):
    return jax.nn.gelu(x, approximate=True)

def _silu(x):
    return jax.nn.silu(x)

def _sigmoid(x):
    return jax.nn.sigmoid(x)

def _layernorm(x, axis=-1, eps=1e-05):
    m = jnp.mean(x, axis=axis, keepdims=True)
    v = jnp.var(x, axis=axis, keepdims=True)
    return (x - m) / jnp.sqrt(v + eps)

def _scatter_add(tgt, idx, src, axis=0):
    return tgt.at[idx].add(src)

def _segment_sum(src, seg, n):
    return jax.ops.segment_sum(src, seg, n)
kernel_name = 'mk_xattn_ffn_d1_seqx_r8_1d90e1'

def setup_inputs(seed: int=0):
    np.random.seed(seed)
    _w = jnp.asarray

    def _rec_inputs():
        import jax
        import jax.numpy as jnp
        _rk = jax.random.key(seed)
        x = 0.5 + 0.2887 * jax.random.normal(jax.random.fold_in(_rk, 1), (4, 256, 256), jnp.float32)
        _lenS = 256 - jax.random.randint(jax.random.fold_in(_rk, 7), (4,), 0, max(1, 256 // 4) + 1, jnp.int32)
        _lenS2 = 256 - jax.random.randint(jax.random.fold_in(_rk, 8), (4,), 0, max(1, 256 // 4) + 1, jnp.int32)
        _ctx_512P = jax.random.normal(jax.random.fold_in(_rk, 11), (4, 16, 64), jnp.float32)
        _ctx_512c = jax.random.dirichlet(jax.random.fold_in(_rk, 511), 0.3 * jnp.ones((16,), jnp.float32), (4, 256))
        _ctx_512t = jnp.einsum('bsk,bkd->bsd', _ctx_512c, _ctx_512P)
        _ctx_512t = _ctx_512t * jax.lax.rsqrt(jnp.mean(jnp.square(_ctx_512t)) + 1e-12) * 0.953939
        ctx_512 = 7.22013e-05 + 1.00017 * (_ctx_512t + 0.3 * jax.random.normal(jax.random.fold_in(_rk, 611), (4, 256, 64), jnp.float32))
        _validS = jnp.arange(256)[None, :] < _lenS[:, None]
        _validS2 = jnp.arange(256)[None, :] < _lenS2[:, None]
        _causal = jnp.tril(jnp.ones((256, 256), dtype=bool))
        mask_SxS2_bk1 = jnp.broadcast_to(_validS2[0:1, :], (256, 256))
        mask_BxS2_bf0 = jnp.logical_not(jnp.ones((4, 256), dtype=bool))
        return (x, ctx_512, mask_SxS2_bk1, mask_BxS2_bf0)
    x, ctx_512, mask_SxS2_bk1, mask_BxS2_bf0 = _rec_inputs()

    def _L0_xattn_setup():
        import jax, jax.numpy as jnp
        import numpy as np
        B, S, H = (8, 256, 64)
        key = jax.random.key(seed)
        kq, kk, kqc, kwq, kwk = jax.random.split(key, 5)
        q = jax.random.normal(kq, (B, S, H), dtype=jnp.float32)
        k = jax.random.normal(kk, (B, S, H), dtype=jnp.float32)
        qc_score = jax.random.uniform(kqc, (B, S, S), dtype=jnp.float32)
        attn_mask = jnp.triu(jnp.ones((S, S), dtype=bool), k=1)
        key_padding_mask = jnp.zeros((B, S), dtype=bool)
        scale = 1.0 / np.sqrt(H)
        Wq = jax.random.normal(kwq, (H, H), dtype=jnp.float32) * scale
        Wk = jax.random.normal(kwk, (H, H), dtype=jnp.float32) * scale
        bq = jnp.zeros((H,), dtype=jnp.float32)
        bk = jnp.zeros((H,), dtype=jnp.float32)
        return {'q': q, 'k': k, 'attn_mask': attn_mask, 'key_padding_mask': key_padding_mask, 'qc_score': qc_score, 'Wq': Wq, 'bq': bq, 'Wk': Wk, 'bk': bk}
    _L0_xattn_all = _L0_xattn_setup()
    _L0_xattn_in = {k: v for k, v in _L0_xattn_all.items() if k in ('Wq', 'bq', 'Wk', 'bk')}
    del _L0_xattn_all

    def _L0_ffn_setup():
        import jax, jax.numpy as jnp
        import numpy as np
        B, T, D, E, F, K, ND = (2, 32, 256, 64, 64, 4, 4)
        H = F * K
        N_SHARED = 2
        key = jax.random.key(seed)
        ks = jax.random.split(key, 12)
        s = lambda k, shape: jax.random.normal(k, shape, jnp.float32) * 0.02
        x = jax.random.normal(ks[0], (B, T, D), jnp.float32)
        Wr = s(ks[1], (E, D))
        router_bias = jnp.zeros((E,), jnp.float32)
        affinity = s(ks[2], (E, ND))
        te_W1 = s(ks[3], (D // 2, D))
        te_b1 = jnp.zeros((D // 2,), jnp.float32)
        te_W2 = s(ks[4], (ND, D // 2))
        te_b2 = jnp.zeros((ND,), jnp.float32)
        Wg = s(ks[5], (E, D, F))
        Wu = s(ks[6], (E, D, F))
        Wd = s(ks[7], (E, F, D))
        Sg = s(ks[8], (N_SHARED, D, H))
        Su = s(ks[9], (N_SHARED, D, H))
        Sd = s(ks[10], (N_SHARED, H, D))
        return dict(x=x, Wr=Wr, router_bias=router_bias, affinity=affinity, te_W1=te_W1, te_b1=te_b1, te_W2=te_W2, te_b2=te_b2, Wg=Wg, Wu=Wu, Wd=Wd, Sg=Sg, Su=Su, Sd=Sd)
    _L0_ffn_all = _L0_ffn_setup()
    _L0_ffn_in = {k: v for k, v in _L0_ffn_all.items() if k in ('Wr', 'router_bias', 'affinity', 'te_W1', 'te_b1', 'te_W2', 'te_b2', 'Wg', 'Wu', 'Wd', 'Sg', 'Su', 'Sd')}
    del _L0_ffn_all
    return {'x': x, 'ctx_512': ctx_512, 'mask_SxS2_bk1': mask_SxS2_bk1, 'mask_BxS2_bf0': mask_BxS2_bf0, 'L0_xattn_Wq': _L0_xattn_in['Wq'], 'L0_xattn_bq': _L0_xattn_in['bq'], 'L0_xattn_Wk': _L0_xattn_in['Wk'], 'L0_xattn_bk': _L0_xattn_in['bk'], 'L0_ffn_Wr': _L0_ffn_in['Wr'], 'L0_ffn_router_bias': _L0_ffn_in['router_bias'], 'L0_ffn_affinity': _L0_ffn_in['affinity'], 'L0_ffn_te_W1': _L0_ffn_in['te_W1'], 'L0_ffn_te_b1': _L0_ffn_in['te_b1'], 'L0_ffn_te_W2': _L0_ffn_in['te_W2'], 'L0_ffn_te_b2': _L0_ffn_in['te_b2'], 'L0_ffn_Wg': _L0_ffn_in['Wg'], 'L0_ffn_Wu': _L0_ffn_in['Wu'], 'L0_ffn_Wd': _L0_ffn_in['Wd'], 'L0_ffn_Sg': _L0_ffn_in['Sg'], 'L0_ffn_Su': _L0_ffn_in['Su'], 'L0_ffn_Sd': _L0_ffn_in['Sd']}

def reference(x, ctx_512, mask_SxS2_bk1, mask_BxS2_bf0, L0_xattn_Wq, L0_xattn_bq, L0_xattn_Wk, L0_xattn_bk, L0_ffn_Wr, L0_ffn_router_bias, L0_ffn_affinity, L0_ffn_te_W1, L0_ffn_te_b1, L0_ffn_te_W2, L0_ffn_te_b2, L0_ffn_Wg, L0_ffn_Wu, L0_ffn_Wd, L0_ffn_Sg, L0_ffn_Su, L0_ffn_Sd):
    import jax
    import jax.numpy as jnp

    def _L0_xattn_ref(q, k, attn_mask, key_padding_mask, qc_score, Wq, bq, Wk, bk):
        import jax, jax.numpy as jnp
        import numpy as np
        B, S, H = (8, 256, 64)
        qp = jnp.einsum('bsh,oh->bso', q, Wq) + bq
        kp = jnp.einsum('bth,oh->bto', k, Wk) + bk
        scaling = jnp.asarray(float(H) ** (-0.5), dtype=qp.dtype)
        scores = jnp.einsum('bsh,bth->bst', qp, kp) * scaling
        scores = scores * qc_score
        mask = attn_mask[None, :, :] | key_padding_mask[:, None, :]
        scores = jnp.where(mask, -jnp.inf, scores)
        return jax.nn.softmax(scores, axis=-1)

    def _L0_ffn_ref(x, Wr, router_bias, affinity, te_W1, te_b1, te_W2, te_b2, Wg, Wu, Wd, Sg, Su, Sd):
        import jax, jax.numpy as jnp
        import numpy as np
        B, T, D, E, F, K, ND = (2, 32, 256, 64, 64, 4, 4)
        H = F * K
        N_SHARED = 2
        b, t, d = x.shape
        n = b * t
        flat = x.reshape(n, d)
        xm = x.mean(axis=1)
        h1 = jax.nn.gelu(xm @ te_W1.T + te_b1, approximate=False)
        task_dist = jax.nn.softmax(h1 @ te_W2.T + te_b2, axis=-1)
        dom = task_dist @ affinity.T
        logits = (flat @ Wr.T).reshape(b, t, E) + 0.5 * dom[:, None, :]
        logits = logits.reshape(n, E)
        scores = jax.nn.softmax(logits, axis=-1)
        _, topk_idx = jax.lax.top_k(logits + router_bias, K)
        topk_scores = jnp.take_along_axis(scores, topk_idx, axis=-1)
        topk_scores = topk_scores / (topk_scores.sum(-1, keepdims=True) + 1e-08)
        combine = jnp.zeros((n, E), x.dtype).at[jnp.arange(n)[:, None], topk_idx].add(topk_scores)
        g = jnp.einsum('nd,edf->enf', flat, Wg)
        u = jnp.einsum('nd,edf->enf', flat, Wu)
        h = jax.nn.silu(g) * u
        hw = h * combine.T[:, :, None]
        out = jnp.einsum('enf,efd->nd', hw, Wd)
        for i in range(Sg.shape[0]):
            sh = jax.nn.silu(flat @ Sg[i]) * (flat @ Su[i])
            out = out + sh @ Sd[i]
        return out.reshape(b, t, d)
    x = x + _L0_xattn_ref(ctx_512, ctx_512, mask_SxS2_bk1, mask_BxS2_bf0, _layernorm(x, axis=-1), L0_xattn_Wq, L0_xattn_bq, L0_xattn_Wk, L0_xattn_bk)
    x = x + _L0_ffn_ref(_layernorm(x, axis=-1), L0_ffn_Wr, L0_ffn_router_bias, L0_ffn_affinity, L0_ffn_te_W1, L0_ffn_te_b1, L0_ffn_te_W2, L0_ffn_te_b2, L0_ffn_Wg, L0_ffn_Wu, L0_ffn_Wd, L0_ffn_Sg, L0_ffn_Su, L0_ffn_Sd)
    return x

_drawn_inputs = setup_inputs


def setup_inputs(seed=0):
    import zlib

    import numpy as np

    out = dict(_drawn_inputs(seed))
    spreads = {'L0_xattn_bq': (0.0, 0.8),
     'L0_xattn_bk': (0.0, 0.8),
     'L0_ffn_router_bias': (0.0, 0.8),
     'L0_ffn_te_b1': (0.0, 2.0),
     'L0_ffn_te_b2': (0.0, 2.0)}
    factors = {'L0_ffn_Wr': 7.691,
     'L0_ffn_affinity': 8.0,
     'L0_ffn_te_W1': 182.265,
     'L0_ffn_te_W2': 8.0,
     'L0_ffn_Wg': 7.189,
     'L0_ffn_Wu': 7.097,
     'L0_ffn_Wd': 7.109,
     'L0_ffn_Sg': 6.796,
     'L0_ffn_Su': 6.7,
     'L0_ffn_Sd': 6.72}
    for name, (base, spread) in spreads.items():
        noise = np.random.default_rng([zlib.crc32(name.encode()), seed]).standard_normal(out[name].shape)
        drawn = base * np.exp(spread * noise) if base else spread * noise
        out[name] = jnp.asarray(drawn.astype(out[name].dtype))
    for name, factor in factors.items():
        out[name] = (out[name] * factor).astype(out[name].dtype)
    return out
```

```python
from contextlib import ExitStack

import concourse.bass as bass
from concourse import mybir

F32 = mybir.dt.float32
BF16 = mybir.dt.bfloat16
I32 = mybir.dt.int32
U32 = mybir.dt.uint32
U8 = mybir.dt.uint8
ALU = mybir.AluOpType
ACT = mybir.ActivationFunctionType
AX = mybir.AxisListType

P = 128
B, S, D = 4, 256, 256
H = 64
E, F, K, ND = 64, 64, 4, 4
NSH, HSH = 2, 256
N = B * S
NT = N // P
TPB = S // P
DC = D // P
HALF = P // 2
NMAIN = E // 2
NOVER = N * K // P
NPAIR = NMAIN + NOVER
SLOTS = NPAIR * P
NJ = NT * K
BIG = 1e30
SENTINEL = -3e38
CHOSEN = 3e38
ROUND = 12582912.0
SKIP = 5001.0
EPS = 1e-5

RING = 4
NG = 4
NY = 3
NC = 8
UNITS = NSH * DC * 2
EARLY = 5


def build_xattn_moe(nc, x, proj, amask, kmask, router, task, b2, rbias, shared, wgu, wd, out):
    z_dram = nc.dram_tensor("z_rows", (N, D), F32, kind="Internal").ap()
    y_dram = nc.dram_tensor("y_slots", (SLOTS, D), F32, kind="Internal").ap()

    with ExitStack() as ctx:
        def sb(name, shape, dt=F32):
            return ctx.enter_context(nc.sbuf_tensor(name, shape, dt))

        def sem(name):
            return ctx.enter_context(nc.semaphore(name))

        wgu_sb = sb("wgu_sb", [P, E, DC, 2 * F])
        wd_sb = sb("wd_sb", [P, NMAIN, D])
        ring_gu = sb("ring_gu", [P, RING, 2, DC, 2 * F])
        ring_d = sb("ring_d", [P, RING, D])
        shared_sb = sb("shared_sb", [P, NSH * 2 * DC * HSH + NSH * DC * D])
        sgu_sb = shared_sb[:, 0:NSH * 2 * DC * HSH].rearrange("p (i g c h) -> p i g c h", i=NSH, g=2, c=DC)
        sd_sb = shared_sb[:, NSH * 2 * DC * HSH:].rearrange("p (q d) -> p q d", d=D)
        proj_sb = sb("proj_sb", [P, N + 2 * H + 2])
        router_sb = sb("router_sb", [P, DC * E + DC * P + ND + 1])
        wr_sb = router_sb[:, 0:DC * E].rearrange("p (c e) -> p c e", c=DC)
        te1_sb = router_sb[:, DC * E:DC * (E + P)].rearrange("p (c j) -> p c j", c=DC)
        te2_sb = router_sb[:, DC * (E + P):DC * (E + P) + ND]
        b1_sb = router_sb[:, DC * (E + P) + ND:]
        aff_sb = sb("aff_sb", [ND, E])
        b2_sb = sb("b2_sb", [B, ND])
        rb_sb = sb("rb_sb", [P, E])
        amask_sb = sb("amask_sb", [P, TPB, S], U8)
        kmask_sb = sb("kmask_sb", [P, B * S], U8)

        xs = sb("xs", [P, NT, D])
        z = sb("z", [P, NT, D])
        zT = sb("zT", [P, DC, N])
        hsh = sb("hsh", [P, NSH * DC, N])
        qc = hsh[:, 0:2, :].rearrange("p a n -> p (a n)").rearrange("p (i d) -> p i d", d=D)
        mb = hsh[:, 2:4, :].rearrange("p a (b s) -> p a b s", b=B)
        qkT = sb("qkT", [P, 2, N])
        sgu_v = qkT[:, :, :].rearrange("p a (r n) -> p a r n", r=2)
        sc = sb("sc", [P, 2, TPB, S])
        xg = sb("xg", [P, NG, D])
        xgT = sb("xgT", [P, 2, DC, P])
        sg = sb("sg", [HALF, 2, P])
        hT = sb("hT", [P, 2, P])
        ysb = sb("ysb", [P, NY, D])

        ident = sb("ident", [P, P])
        ones_bf = sb("ones_bf", [P, P], BF16)
        tri = sb("tri", [P, P], BF16)
        tri64i = sb("tri64i", [E, E], BF16)
        lanes = sb("lanes", [P, P], BF16)
        lanes_f = sb("lanes_f", [E, E])
        row_no = sb("row_no", [P, 1], I32)
        e_main = sb("e_main", [P, E])
        e_over = sb("e_over", [P, E])

        st = sb("st", [P, NT, 6])
        mv1 = sb("mv1", [P, NT, 2])
        mv2 = sb("mv2", [P, NT, 2])
        rstd1 = sb("rstd1", [P, NT])
        rstd2 = sb("rstd2", [P, NT])
        veps = sb("veps", [P, 2, NT])
        mhalf = sb("mhalf", [P, NT])
        smax = sb("smax", [P, NT])
        nmax = sb("nmax", [P, NT])
        ssum = sb("ssum", [P, NT])
        skeep = sb("skeep", [P, NT])
        rinv = sb("rinv", [P, NT])
        zsum = sb("zsum", [P, DC, B])
        h1 = sb("h1", [P, B])
        tl = sb("tl", [B, 4, ND])
        ts_ = sb("ts_", [B, 4])
        tdb = sb("tdb", [ND, B, P])
        lb = proj_sb[:, 0:NT * (E + 4)].rearrange("p (i e) -> p i e", i=NT)
        marked = proj_sb[:, NT * (E + 4):2 * NT * (E + 4)].rearrange("p (i e) -> p i e", i=NT)
        top8 = sb("top8", [P, NT, 8])
        chosen = sb("chosen", [P, NT, E], BF16)
        logit = sb("logit", [P, NT, E])
        lmax = sb("lmax", [P, NT])
        over = sc[:, 0, :, :].rearrange("p c s -> p (c s)").rearrange("p (i e) -> p i e", e=E)
        slotmap = sb("slotmap", [P, NT, E])
        halves = sb("halves", [E, 3, P])
        halves_bf = sb("halves_bf", [E, P], BF16)
        d_over = sb("d_over", [P, E])
        slot8 = sb("slot8", [P, NT, 8])
        slot_i = sb("slot_i", [P, 3, NJ], I32)
        oh_lane = sb("oh_lane", [P, 4, P], BF16)
        oh_tile = sb("oh_tile", [P, 4, 2, NPAIR], BF16)
        lsum = sb("lsum", [P, 2, NPAIR])
        tok = sb("tok", [P, NPAIR], U32)
        cuml = sb("cuml", [E, 1])
        cmp = sb("cmp", [E, E], BF16)
        half_e = sb("half_e", [1, E], I32)
        pick = sb("pick", [P, NJ])
        junk = sc[:, 1, :, :].rearrange("p c s -> p (c s)").rearrange("p (n e) -> p n e", e=E)
        zden = sb("zden", [P, 3, NT])
        wgt = sb("wgt", [P, NJ])

        pb = [ctx.enter_context(nc.psum_tensor(f"pb{i}", [P, 512], F32)) for i in range(8)]

        ld_proj, ld_mask, ld_router = sem("ld_proj"), sem("ld_mask"), sem("ld_router")
        ld_task, ld_b2, ld_rb, ld_shared, ld_kmask = sem("ld_task"), sem("ld_b2"), sem("ld_rb"), sem("ld_shared"), sem("ld_kmask")
        ld_x = [sem(f"ld_x{b}") for b in range(B)]
        ld_gu = [sem(f"ld_gu{n}") for n in range(8)]
        ld_d = [sem(f"ld_d{n}") for n in range(4)]
        ring_in = [sem(f"ring_in{r}") for r in range(RING)]
        const_ok, mask_ok = sem("const_ok"), sem("mask_ok")
        proj_ps, q_sb, k_sb = sem("proj_ps"), sem("q_sb"), sem("k_sb")
        stat1, var1, rstd1_ok, qc_ok = sem("stat1"), sem("var1"), sem("rstd1_ok"), sem("qc_ok")
        score_ps, score_x, score_m, nmax_ok, exp_ok = (sem("score_ps"), sem("score_x"), sem("score_m"), sem("nmax_ok"), sem("exp_ok"))
        keep_ok, rinv_ok, x1_ok = sem("keep_ok"), sem("rinv_ok"), sem("x1_ok")
        stat2, mv2_ok, var2, rstd2_ok, z_ok = sem("stat2"), sem("mv2_ok"), sem("var2"), sem("rstd2_ok"), sem("z_ok")
        z_out = sem("z_out")
        zT_ps, zT_sb = sem("zT_ps"), sem("zT_sb")
        h1_ps, h1_ok, tl_ps, task_dve, task_exp, td_ps, tdb_ok = (
            sem("h1_ps"), sem("h1_ok"), sem("tl_ps"), sem("task_dve"), sem("task_exp"), sem("td_ps"), sem("tdb_ok"))
        logit_ps, lb_ok, top_ok, cut_ok, marked_ok, chosen_ok = (
            sem("logit_ps"), sem("lb_ok"), sem("top_ok"), sem("cut_ok"), sem("marked_ok"), sem("chosen_ok"))
        rank_ps, count_ps, halves_ok, base_ps, dover_ok, slot_step = (
            sem("rank_ps"), sem("count_ps"), sem("halves_ok"), sem("base_ps"), sem("dover_ok"), sem("slot_step"))
        slot8_ok, slotf, onehot, listed, tok_step = (
            sem("slot8_ok"), sem("slotf"), sem("onehot"), sem("listed"), sem("tok_step"))
        cmp_ok, half_ps, half_ok = sem("cmp_ok"), sem("half_ps"), sem("half_ok")
        logit_sb, lmax_ok, lsub_ok, lexp_ok = sem("logit_sb"), sem("lmax_ok"), sem("lsub_ok"), sem("lexp_ok")
        unit_ps, unit_sb, unit_h, unit_h_dve = sem("unit_ps"), sem("unit_sb"), sem("unit_h"), sem("unit_h_dve")
        got = [sem(f"got{n}") for n in range(NG)]
        xT_ps, xT_sb, gu_ps, silu_ok, h_ok, y_ps, y_sb = (
            sem("xT_ps"), sem("xT_sb"), sem("gu_ps"), sem("silu_ok"), sem("h_ok"), sem("y_ps"), sem("y_sb"))
        zeroed = sem("zeroed")
        y_out = [sem(f"y_out{n}") for n in range(NY)]
        back = [sem(f"back{n}") for n in range(NC)]
        pick_ok, w_step = sem("pick_ok"), sem("w_step")
        down_ps, mixed, out_ok = sem("down_ps"), sem("mixed"), sem("out_ok")

        def x_rows(dram, b):
            return dram[b * S:(b + 1) * S, :].rearrange("(c p) d -> p c d", p=P)

        def res(s):
            if s < NMAIN:
                return (lambda a, c: wgu_sb[:, 2 * s + a, c, :]), wd_sb[:, s, :]
            r = (s - NMAIN) % RING
            return (lambda a, c: ring_gu[:, r, a, c, :]), ring_d[:, r, :]

        block = ctx.enter_context(nc.Block())

        @block.sync
        def _(sp):
            sp.dma_start(proj_sb[0:H, :], proj).then_inc(ld_proj, 16)
            sp.dma_start(xs[:, 0:TPB, :], x_rows(x, 0)).then_inc(ld_x[0], 16)
            sp.dma_start(kmask_sb[:, :], kmask.partition_broadcast(P)).then_inc(ld_kmask, 16)
            sp.dma_start(amask_sb[:, :, :], amask.rearrange("(c p) t -> p c t", p=P)).then_inc(ld_mask, 16)
            for b in range(1, B):
                sp.dma_start(xs[:, TPB * b:TPB * (b + 1), :], x_rows(x, b)).then_inc(ld_x[b], 16)
            sp.dma_start(router_sb[:, :], router).then_inc(ld_router, 16)
            sp.dma_start(aff_sb[:, :], task).then_inc(ld_task, 16)
            sp.dma_start(b2_sb[:, :], b2.partition_broadcast(B)).then_inc(ld_b2, 16)
            sp.dma_start(rb_sb[:, :], rbias.partition_broadcast(P)).then_inc(ld_rb, 16)
            sp.dma_start(shared_sb[:, :], shared).then_inc(ld_shared, 16)
            def load_weights(n):
                sp.dma_start(wgu_sb[:, 8 * n:8 * (n + 1), :, :].rearrange("p e c f -> p e (c f)"),
                             wgu[8 * n:8 * (n + 1), :, :].rearrange("e p n -> p e n")).then_inc(ld_gu[n], 16)
                if n % 2 == 0:
                    q = 4 * n
                    sp.dma_start(wd_sb[:, q:q + 8, :],
                                 wd[2 * q:2 * q + 16, :, :].rearrange("(q a) f d -> (a f) q d", a=2)).then_inc(ld_d[n // 2], 16)
            for n in range(4):
                load_weights(n)
            for b in range(B):
                sp.wait_ge(z_ok, TPB * (b + 1))
                sp.dma_start(x_rows(z_dram, b), z[:, TPB * b:TPB * (b + 1), :]).then_inc(z_out, 16)
                load_weights(4 + b)
            sp.wait_ge(half_ok, 1)

            def load_ring(t):
                r = t % RING
                if t >= RING:
                    sp.wait_ge(y_ps, NMAIN + t - RING + 1)
                for a in range(2):
                    e = sp.value_load(half_e[0:1, 2 * t + a:2 * t + a + 1], min_val=0, max_val=E - 1)
                    sp.dma_start(ring_gu[:, r, a, :, :].rearrange("p c f -> p (c f)"),
                                 wgu[bass.ds(e, 1), :, :].rearrange("o p n -> (o p) n")).then_inc(ring_in[r], 16)
                    sp.dma_start(ring_d[a * HALF:(a + 1) * HALF, r, :],
                                 wd[bass.ds(e, 1), :, :].rearrange("o f d -> (o f) d")).then_inc(ring_in[r], 16)

            for t in range(RING):
                load_ring(t)
            for s in range(NPAIR):
                sp.wait_ge(y_sb, s + 1)
                sp.dma_start(y_dram[s * P:(s + 1) * P, :], ysb[:, s % NY, :]).then_inc(y_out[s % NY], 16)
                t = s - NMAIN + RING
                if RING <= t < NOVER:
                    load_ring(t)
            for i in range(NT):
                sp.wait_ge(mixed, (i + 1) * (K + 1))
                sp.dma_start(out[i * P:(i + 1) * P, :], xs[:, i, :]).then_inc(out_ok, 16)
            sp.wait_ge(out_ok, 16 * NT)

        @block.gpsimd
        def _(pool):
            g = nc.gpsimd
            g.memset(mhalf[:, :], -0.5).then_inc(const_ok, 1)
            g.memset(ident[:, :], 0.0).then_inc(const_ok, 1)
            g.memset(ones_bf[:, :], 1.0).then_inc(const_ok, 1)
            g.iota(lanes[:, :], [[1, P]], base=0, channel_multiplier=0, allow_small_or_imprecise_dtypes=True).then_inc(const_ok, 1)
            g.iota(lanes_f[:, :], [[1, E]], base=0, channel_multiplier=0, allow_small_or_imprecise_dtypes=True).then_inc(const_ok, 1)
            g.iota(row_no[:, :], [[1, 1]], base=1, channel_multiplier=1).then_inc(const_ok, 1)
            g.iota(e_main[:, :], [[HALF, E]], base=1, channel_multiplier=0, allow_small_or_imprecise_dtypes=True).then_inc(const_ok, 1)
            g.iota(e_over[:, :], [[-HALF, E]], base=HALF * (2 * NMAIN - 1), channel_multiplier=0, allow_small_or_imprecise_dtypes=True).then_inc(const_ok, 1)
            pool.wait_ge(const_ok, 3)
            g.affine_select(out=ident[:, :], in_=ident[:, :], compare_op=ALU.not_equal, fill=1.0, base=0,
                            pattern=[[-1, P]], channel_multiplier=1).then_inc(const_ok, 1)
            g.affine_select(out=tri[:, :], in_=ones_bf[:, :], compare_op=ALU.is_gt, fill=0.0, base=0,
                            pattern=[[1, P]], channel_multiplier=-1).then_inc(const_ok, 1)
            g.affine_select(out=tri64i[:, :], in_=ones_bf[0:E, 0:E], compare_op=ALU.is_ge, fill=0.0, base=0,
                            pattern=[[1, E]], channel_multiplier=-1).then_inc(const_ok, 1)

            pool.wait_ge(var1, 1)
            g.tensor_tensor(rstd1[:, :], veps[:, 0, :], mhalf[:, :], ALU.pow).then_inc(rstd1_ok, 1)
            for b in range(B):
                pool.wait_ge(var2, b + 1)
                t = slice(TPB * b, TPB * (b + 1))
                g.tensor_tensor(rstd2[:, t], veps[:, 1, t], mhalf[:, t], ALU.pow).then_inc(rstd2_ok, 1)

            pool.wait_ge(lmax_ok, 1)
            g.tensor_tensor(logit[:, :, :], logit[:, :, :], lmax[:, :].unsqueeze(2).broadcast_to([P, NT, E]),
                            ALU.subtract).then_inc(lsub_ok, 1)

            for n in range(EARLY):
                i, hc, blk = n // 4, n // 2 % 2, n % 2
                pool.wait_ge(unit_sb, 2 * n + 2)
                g.tensor_tensor(hsh[:, 2 * i + hc, blk * 512:(blk + 1) * 512], sgu_v[:, 0, n % 2, :], sgu_v[:, 1, n % 2, :],
                                ALU.mult).then_inc(unit_h, 1)

            pool.wait_ge(tok_step, 3)
            pool.wait_ge(z_out, 16 * B)
            pool.wait_ge(zeroed, 1)
            for s in range(NPAIR):
                if s >= NG:
                    pool.wait_ge(xT_ps, s - NG + 1)
                g.indirect_dma_start(xg[:, s % NG, :], None, z_dram,
                                     bass.IndirectOffsetOnAxis(ap=tok[:, s:s + 1], axis=0),
                                     bounds_check=N - 1, oob_is_err=False).then_inc(got[s % NG], 16)
            for n in range(NY):
                pool.wait_ge(y_out[n], 16 * len(range(n, NPAIR, NY)))
            for j in range(NJ):
                if j >= NC:
                    i = (j - NC) // K
                    pool.wait_ge(mixed, i * (K + 1) + 1 + (j - NC) % K + 1)
                g.indirect_dma_start(z[:, j % NC, :], None, y_dram,
                                     bass.IndirectOffsetOnAxis(ap=slot_i[:, 0, j:j + 1].bitcast(U32), axis=0),
                                     bounds_check=SLOTS - 1, oob_is_err=False).then_inc(back[j % NC], 16)

        def evac_zT(act, b):
            act.wait_ge(zT_ps, b + 1)
            for c in range(DC):
                nc.scalar.activation(zT[:, c, b * S:(b + 1) * S], pb[b][:, c * S:(c + 1) * S], ACT.Identity,
                                     accum_out=zsum[:, c, b:b + 1]).then_inc(zT_sb, 1)

        @block.scalar
        def _(act):
            a = nc.scalar
            for blk in range(2):
                act.wait_ge(proj_ps, 2 * blk + 1)
                a.activation(qkT[0:H, 0, blk * 512:(blk + 1) * 512], pb[2 * blk][0:H, :], ACT.Identity,
                             bias=proj_sb[0:H, N + 2 * H:N + 2 * H + 1]).then_inc(q_sb, 1)
            for b in range(B):
                for c in range(TPB):
                    i = TPB * b + c
                    act.wait_ge(nmax_ok, b + 1)
                    a.activation(sc[:, b % 2, c, :], sc[:, b % 2, c, :], ACT.Exp, bias=nmax[:, i:i + 1],
                                 accum_out=ssum[:, i:i + 1]).then_inc(exp_ok, 1)
                if b >= 1:
                    evac_zT(act, b - 1)
            evac_zT(act, B - 1)
            act.wait_ge(h1_ps, 1)
            a.activation(h1[:, :], pb[5][:, 0:B], ACT.Gelu, bias=b1_sb, scale=1.0 / S).then_inc(h1_ok, 1)
            act.wait_ge(task_dve, 3)
            a.activation(tl[:, 1, :], tl[:, 0, :], ACT.Exp, bias=ts_[:, 1:2], accum_out=ts_[:, 2:3]).then_inc(task_exp, 1)
            act.wait_ge(lb_ok, 2)
            a.activation(logit[:, :, :], pb[4][:, :].rearrange("p (i e) -> p i e", e=E), ACT.Identity).then_inc(logit_sb, 1)
            act.wait_ge(lsub_ok, 1)
            a.activation(logit[:, :, :], logit[:, :, :], ACT.Exp).then_inc(lexp_ok, 1)

            def unit(n):
                act.wait_ge(unit_ps, n + 1)
                if 2 <= n < EARLY + 2:
                    act.wait_ge(unit_h, min(n - 1, EARLY))
                if n >= EARLY + 2:
                    act.wait_ge(unit_h_dve, n - 1 - EARLY)
                bank = 2 * (n % 2)
                a.activation(sgu_v[:, 0, n % 2, :], pb[bank][:, :], ACT.Silu).then_inc(unit_sb, 1)
                a.activation(sgu_v[:, 1, n % 2, :], pb[bank + 1][:, :], ACT.Identity).then_inc(unit_sb, 1)

            for n in range(EARLY):
                unit(n)
            for s in range(NPAIR + 4):
                if 1 <= s <= NPAIR:
                    t = s - 1
                    act.wait_ge(gu_ps, t + 1)
                    if t >= 2:
                        act.wait_ge(h_ok, t - 1)
                    a.activation(sg[:, t % 2, :], pb[2 + t % 2][0:HALF, 0:P], ACT.Silu).then_inc(silu_ok, 1)
                if s >= 4:
                    t = s - 4
                    act.wait_ge(y_ps, t + 1)
                    if t >= NY:
                        act.wait_ge(y_out[t % NY], 16 * (t // NY))
                    a.activation(ysb[:, t % NY, :], pb[4 + t % 2][:, 0:D], ACT.Identity).then_inc(y_sb, 1)
            for n in range(EARLY, UNITS):
                unit(n)

        @block.vector
        def _(dve):
            v = nc.vector
            v.memset(xg[:, :, :], 0.0).then_inc(zeroed, 1)
            v.memset(hT[:, :, :], 0.0).then_inc(zeroed, 1)
            for blk in range(2):
                dve.wait_ge(proj_ps, 2 * blk + 2)
                v.tensor_scalar(qkT[0:H, 1, blk * 512:(blk + 1) * 512], pb[2 * blk + 1][0:H, :],
                                proj_sb[0:H, N + 2 * H + 1:N + 2 * H + 2], None, ALU.add).then_inc(k_sb, 1)
            dve.wait_ge(ld_mask, 16)
            dve.wait_ge(ld_kmask, 16)
            for b in range(B):
                v.tensor_tensor(mb[:, :, b, :], amask_sb[:, :, :],
                                kmask_sb[:, b * S:(b + 1) * S].unsqueeze(1).broadcast_to([P, TPB, S]), ALU.max).then_inc(mask_ok, 1)
            for b in range(B):
                dve.wait_ge(ld_x[b], 16)
                for c in range(TPB):
                    i = TPB * b + c
                    v.bn_stats(st[:, i, :], xs[:, i, :]).then_inc(stat1, 1)
            for i in range(NT):
                dve.wait_ge(stat1, i + 1)
                v.bn_aggr(mv1[:, i, :], st[:, i, :]).then_inc(stat1, 1)
            dve.wait_ge(stat1, 2 * NT)
            v.tensor_scalar(veps[:, 0, :], mv1[:, :, 1], EPS, None, ALU.add).then_inc(var1, 1)
            dve.wait_ge(rstd1_ok, 1)
            for i in range(NT):
                v.tensor_scalar(qc[:, i, :], xs[:, i, :], mv1[:, i, 0:1], rstd1[:, i:i + 1], ALU.subtract, ALU.mult).then_inc(qc_ok, 1)

            def scores(b):
                sl = sc[:, b % 2, :, :]
                dve.wait_ge(score_ps, b + 1)
                dve.wait_ge(qc_ok, TPB * (b + 1))
                if b >= 2:
                    dve.wait_ge(x1_ok, TPB * (b - 1))
                v.scalar_tensor_tensor(sl, pb[4 + b][:, :].rearrange("p (c t) -> p c t", c=TPB), float(H) ** -0.5,
                                       qc[:, TPB * b:TPB * (b + 1), :], ALU.mult, ALU.mult).then_inc(score_x, 1)
                dve.wait_ge(score_x, b + 1)
                dve.wait_ge(mask_ok, b + 1)
                t = slice(TPB * b, TPB * (b + 1))
                v.scalar_tensor_tensor(sl, mb[:, :, b, :], -BIG, sl, ALU.mult, ALU.add).then_inc(score_m, 1)
                dve.wait_ge(score_m, 2 * b + 1)
                v.tensor_reduce(smax[:, t], sl, AX.X, ALU.max).then_inc(score_m, 1)
                dve.wait_ge(score_m, 2 * b + 2)
                v.tensor_scalar(nmax[:, t], smax[:, t], -1.0, None, ALU.mult).then_inc(nmax_ok, 1)

            def finish(b):
                t = slice(TPB * b, TPB * (b + 1))
                dve.wait_ge(exp_ok, TPB * (b + 1))
                v.scalar_tensor_tensor(skeep[:, t], smax[:, t], -0.5 * BIG, ssum[:, t], ALU.is_gt, ALU.mult).then_inc(keep_ok, 1)
                dve.wait_ge(keep_ok, b + 1)
                v.reciprocal(rinv[:, t], skeep[:, t]).then_inc(rinv_ok, 1)
                dve.wait_ge(rinv_ok, b + 1)
                for c in range(TPB):
                    i = TPB * b + c
                    v.scalar_tensor_tensor(xs[:, i, :], sc[:, b % 2, c, :], rinv[:, i:i + 1], xs[:, i, :],
                                           ALU.mult, ALU.add).then_inc(x1_ok, 1)
                for c in range(TPB):
                    i = TPB * b + c
                    dve.wait_ge(x1_ok, i + 1)
                    v.bn_stats(st[:, i, :], xs[:, i, :]).then_inc(stat2, 1)
                for c in range(TPB):
                    i = TPB * b + c
                    dve.wait_ge(stat2, i + 1)
                    v.bn_aggr(mv2[:, i, :], st[:, i, :]).then_inc(mv2_ok, 1)
                dve.wait_ge(mv2_ok, TPB * (b + 1))
                v.tensor_scalar(veps[:, 1, t], mv2[:, t, 1], EPS, None, ALU.add).then_inc(var2, 1)

            def normalise(b):
                dve.wait_ge(rstd2_ok, b + 1)
                for c in range(TPB):
                    i = TPB * b + c
                    v.tensor_scalar(z[:, i, :], xs[:, i, :], mv2[:, i, 0:1], rstd2[:, i:i + 1],
                                    ALU.subtract, ALU.mult).then_inc(z_ok, 1)

            scores(0)
            scores(1)
            finish(0)
            for b in range(2, B):
                scores(b)
                normalise(b - 2)
                finish(b - 1)
            normalise(B - 2)
            finish(B - 1)
            normalise(B - 1)

            v.memset(lb[:, :, E:E + 4], SENTINEL).then_inc(lb_ok, 1)
            dve.wait_ge(tl_ps, 1)
            dve.wait_ge(ld_b2, 16)
            v.tensor_tensor(tl[:, 0, :], pb[5][0:B, 16:16 + ND], b2_sb[:, :], ALU.add).then_inc(task_dve, 1)
            dve.wait_ge(task_dve, 1)
            v.tensor_reduce(ts_[:, 0:1], tl[:, 0, :], AX.X, ALU.max).then_inc(task_dve, 1)
            dve.wait_ge(task_dve, 2)
            v.tensor_scalar(ts_[:, 1:2], ts_[:, 0:1], -1.0, None, ALU.mult).then_inc(task_dve, 1)
            dve.wait_ge(task_exp, 1)
            v.reciprocal(ts_[:, 3:4], ts_[:, 2:3]).then_inc(task_dve, 1)
            dve.wait_ge(task_dve, 4)
            v.tensor_scalar(tl[:, 2, :], tl[:, 1, :], ts_[:, 3:4], 0.5, ALU.mult, ALU.mult).then_inc(task_dve, 1)
            dve.wait_ge(td_ps, 1)
            v.tensor_copy(tdb[:, :, :], pb[5][0:ND, 32:32 + B].unsqueeze(2).broadcast_to([ND, B, P])).then_inc(tdb_ok, 1)

            dve.wait_ge(logit_ps, 1)
            dve.wait_ge(ld_rb, 16)
            lg = pb[4][:, :].rearrange("p (i e) -> p i e", e=E)
            v.tensor_tensor(lb[:, :, 0:E], lg, rb_sb[:, :].unsqueeze(1).broadcast_to([P, NT, E]), ALU.add).then_inc(lb_ok, 1)
            dve.wait_ge(lb_ok, 2)
            for i in range(NT):
                v.max(top8[:, i, :], lb[:, i, :]).then_inc(top_ok, 1)
            dve.wait_ge(top_ok, NT)
            v.memset(top8[:, :, K:8], SENTINEL).then_inc(cut_ok, 1)
            dve.wait_ge(cut_ok, 1)
            for i in range(NT):
                v.match_replace(marked[:, i, :], top8[:, i, :], lb[:, i, :], CHOSEN).then_inc(marked_ok, 1)
            dve.wait_ge(marked_ok, NT)
            v.tensor_scalar(chosen[:, :, :], marked[:, :, 0:E], CHOSEN, None, ALU.is_ge).then_inc(chosen_ok, 1)

            dve.wait_ge(logit_sb, 1)
            v.tensor_reduce(lmax[:, :], logit[:, :, :], AX.X, ALU.max).then_inc(lmax_ok, 1)
            dve.wait_ge(count_ps, 1)
            v.tensor_scalar(halves[:, 0, :], pb[6][0:E, 0:P], 1.0 / HALF, -1.0 / HALF - 0.5 + 0.5 / HALF, ALU.mult, ALU.add).then_inc(halves_ok, 1)
            dve.wait_ge(halves_ok, 1)
            v.tensor_scalar(halves[:, 1, :], halves[:, 0, :], ROUND, None, ALU.add).then_inc(halves_ok, 1)
            dve.wait_ge(halves_ok, 2)
            v.tensor_scalar(halves_bf[:, :], halves[:, 1, :], -ROUND, 0.0, ALU.add, ALU.max).then_inc(halves_ok, 1)
            rk = pb[7][:, :].rearrange("p (i e) -> p i e", e=E)
            dve.wait_ge(rank_ps, 1)
            v.tensor_tensor(slotmap[:, :, :], rk, e_main[:, :].unsqueeze(1).broadcast_to([P, NT, E]), ALU.add).then_inc(slot_step, 1)
            dve.wait_ge(base_ps, 1)
            v.scalar_tensor_tensor(d_over[:, :], pb[5][:, 64:64 + E], float(HALF), e_over[:, :], ALU.mult, ALU.add).then_inc(dover_ok, 1)
            dve.wait_ge(dover_ok, 1)
            v.scalar_tensor_tensor(over, rk, float(HALF), d_over[:, :].unsqueeze(1).broadcast_to([P, NT, E]),
                                   ALU.is_ge, ALU.mult).then_inc(slot_step, 1)
            dve.wait_ge(slot_step, 2)
            v.tensor_tensor(slotmap[:, :, :], slotmap[:, :, :], over, ALU.add).then_inc(slot_step, 1)
            dve.wait_ge(slot_step, 3)
            v.tensor_tensor(slotmap[:, :, :], slotmap[:, :, :], chosen[:, :, :], ALU.mult).then_inc(slot_step, 1)
            dve.wait_ge(slot_step, 4)
            for i in range(NT):
                v.max(slot8[:, i, :], slotmap[:, i, :]).then_inc(slot8_ok, 1)
            dve.wait_ge(slot8_ok, NT)
            v.tensor_scalar(slot_i[:, 0, :].rearrange("p (i k) -> p i k", k=K), slot8[:, :, 0:K], -1.0, None, ALU.add).then_inc(slotf, 1)
            dve.wait_ge(slotf, 1)
            v.tensor_scalar(slot_i[:, 1, :], slot_i[:, 0, :], P - 1, None, ALU.bitwise_and).then_inc(slotf, 1)
            v.tensor_scalar(slot_i[:, 2, :], slot_i[:, 0, :], 7, None, ALU.logical_shift_right).then_inc(slotf, 1)
            dve.wait_ge(slotf, 3)
            for j in range(NJ):
                if j >= 4:
                    dve.wait_ge(listed, j - 3)
                v.tensor_scalar(oh_lane[:, j % 4, :], lanes[:, :], slot_i[:, 1, j:j + 1], None, ALU.is_equal).then_inc(onehot, 1)
                v.tensor_scalar(oh_tile[:, j % 4, 0, :], lanes[:, 0:NPAIR], slot_i[:, 2, j:j + 1], row_no[:, :],
                                ALU.is_equal, ALU.mult).then_inc(onehot, 1)
                v.tensor_scalar(oh_tile[:, j % 4, 1, :], lanes[:, 0:NPAIR], slot_i[:, 2, j:j + 1], float(P * (j // K)),
                                ALU.is_equal, ALU.mult).then_inc(onehot, 1)
            dve.wait_ge(listed, NJ)
            v.tensor_scalar(lsum[:, 0, :], pb[6][:, 128:128 + NPAIR], 0.0, SKIP, ALU.is_equal, ALU.mult).then_inc(tok_step, 1)
            dve.wait_ge(tok_step, 1)
            v.tensor_tensor(lsum[:, 1, :], pb[6][:, 128 + NPAIR:128 + 2 * NPAIR], lsum[:, 0, :], ALU.add).then_inc(tok_step, 1)
            dve.wait_ge(tok_step, 2)
            v.scalar_tensor_tensor(tok[:, :], pb[6][:, 128:128 + NPAIR], -1.0, lsum[:, 1, :], ALU.add, ALU.add).then_inc(tok_step, 1)
            dve.wait_ge(base_ps, 1)
            v.tensor_copy(cuml[:, :], pb[5][0:E, 128:129]).then_inc(cmp_ok, 1)
            dve.wait_ge(cmp_ok, 1)
            v.tensor_scalar(cmp[:, :], lanes_f[:, :], cuml[:, :], None, ALU.is_ge).then_inc(cmp_ok, 1)
            dve.wait_ge(half_ps, 1)
            v.tensor_scalar(half_e[:, :], pb[5][0:1, 192:192 + E], float(E - 1), None, ALU.min).then_inc(half_ok, 1)

            def weights_of_choices():
                dve.wait_ge(lexp_ok, 1)
                v.tensor_reduce(zden[:, 0, :], logit[:, :, :], AX.X, ALU.add).then_inc(w_step, 1)
                for j in range(NJ):
                    i, k = j // K, j % K
                    if j >= 4:
                        dve.wait_ge(pick_ok, j - 3)
                    v.scalar_tensor_tensor(junk[:, j % 4, :], slotmap[:, i, :], slot8[:, i, k:k + 1], logit[:, i, :],
                                           ALU.is_equal, ALU.mult, accum_out=pick[:, j:j + 1]).then_inc(pick_ok, 1)
                dve.wait_ge(pick_ok, NJ)
                pk = pick[:, :].rearrange("p (i k) -> p i k", k=K)
                v.tensor_reduce(zden[:, 1, :], pk, AX.X, ALU.add).then_inc(w_step, 1)
                dve.wait_ge(w_step, 2)
                v.scalar_tensor_tensor(zden[:, 2, :], zden[:, 0, :], 1e-8, zden[:, 1, :], ALU.mult, ALU.add).then_inc(w_step, 1)
                dve.wait_ge(w_step, 3)
                v.reciprocal(zden[:, 0, :], zden[:, 2, :]).then_inc(w_step, 1)
                dve.wait_ge(w_step, 4)
                v.tensor_tensor(wgt[:, :].rearrange("p (i k) -> p i k", k=K), pk,
                                zden[:, 0, :].unsqueeze(2).broadcast_to([P, NT, K]), ALU.mult).then_inc(w_step, 1)

            dve.wait_ge(zeroed, 2)
            for s in range(NPAIR + 2):
                if s < NPAIR:
                    dve.wait_ge(xT_ps, s + 1)
                    if s >= 2:
                        dve.wait_ge(gu_ps, s - 1)
                    v.tensor_copy(xgT[:, s % 2, :, :], pb[s % 2][:, 0:D].rearrange("p (c n) -> p c n", c=DC)).then_inc(xT_sb, 1)
                if s >= 2:
                    t = s - 2
                    dve.wait_ge(silu_ok, t + 1)
                    if t >= 2:
                        dve.wait_ge(y_ps, t - 1)
                    for a in range(2):
                        n = slice(a * HALF, (a + 1) * HALF)
                        ins = v.tensor_tensor(hT[n, t % 2, n], sg[:, t % 2, n], pb[2 + t % 2][HALF:P, n], ALU.mult)
                    ins.then_inc(h_ok, 1)
                if s == NMAIN:
                    weights_of_choices()
            for n in range(EARLY, UNITS):
                i, hc, blk = n // 4, n // 2 % 2, n % 2
                dve.wait_ge(unit_sb, 2 * n + 2)
                v.tensor_tensor(hsh[:, 2 * i + hc, blk * 512:(blk + 1) * 512], sgu_v[:, 0, n % 2, :], sgu_v[:, 1, n % 2, :],
                                ALU.mult).then_inc(unit_h_dve, 1)
            dve.wait_ge(w_step, 5)
            for i in range(NT):
                n = i * (K + 1)
                dve.wait_ge(down_ps, i + 1)
                v.tensor_tensor(xs[:, i, :], pb[4 + i % 2][:, 0:D], xs[:, i, :], ALU.add).then_inc(mixed, 1)
                for k in range(K):
                    j = i * K + k
                    dve.wait_ge(back[j % NC], 16 * (j // NC + 1))
                    dve.wait_ge(mixed, n + 1 + k)
                    v.scalar_tensor_tensor(xs[:, i, :], z[:, j % NC, :], wgt[:, j:j + 1], xs[:, i, :],
                                           ALU.mult, ALU.add).then_inc(mixed, 1)

        @block.tensor
        def _(pe):
            t = nc.tensor
            pe.wait_ge(ld_proj, 16)
            for blk in range(2):
                for w in range(2):
                    t.matmul(pb[2 * blk + w][0:H, :], proj_sb[0:H, N + w * H:N + (w + 1) * H],
                             proj_sb[0:H, blk * 512:(blk + 1) * 512], start=True, stop=True).then_inc(proj_ps, 1)
            for b in range(B):
                pe.wait_ge(q_sb, b // 2 + 1)
                pe.wait_ge(k_sb, b // 2 + 1)
                for c in range(TPB):
                    q0 = b * S + c * P
                    ins = t.matmul(pb[4 + b][:, c * S:(c + 1) * S], qkT[0:H, 0, q0:q0 + P], qkT[0:H, 1, b * S:(b + 1) * S],
                                   start=True, stop=True)
                ins.then_inc(score_ps, 1)
            pe.wait_ge(const_ok, 11)

            def logits(b):
                pe.wait_ge(zT_sb, DC * (b + 1))
                if b == 0:
                    pe.wait_ge(ld_router, 16)
                    pe.wait_ge(score_x, 1)
                for c in range(TPB):
                    i = TPB * b + c
                    for h in range(DC):
                        t.matmul(pb[4][:, i * E:(i + 1) * E], zT[:, h, i * P:(i + 1) * P], wr_sb[:, h, :],
                                 start=(i == 0 and h == 0), stop=False, skip_group_check=True)

            for b in range(B):
                pe.wait_ge(z_ok, TPB * (b + 1))
                for h in range(DC):
                    for c in range(TPB):
                        i = TPB * b + c
                        ins = t.transpose(pb[b][:, h * S + c * P:h * S + (c + 1) * P], z[:, i, h::DC], ident[:, :])
                ins.then_inc(zT_ps, 1)
                if b >= 1:
                    logits(b - 1)
            pe.wait_ge(zT_sb, DC * B)
            pe.wait_ge(score_x, B)
            for h in range(DC):
                ins = t.matmul(pb[5][:, 0:B], te1_sb[:, h, :], zsum[:, h, :], start=(h == 0), stop=(h == DC - 1))
            ins.then_inc(h1_ps, 1)
            logits(B - 1)

            def unit(n):
                i, hc, blk = n // 4, n // 2 % 2, n % 2
                if n == 0:
                    pe.wait_ge(ld_shared, 16)
                if n >= 2:
                    pe.wait_ge(unit_sb, 2 * (n - 1))
                for g in range(2):
                    for h in range(DC):
                        ins = t.matmul(pb[2 * (n % 2) + g][:, :], sgu_sb[:, i, g, h, hc * P:(hc + 1) * P],
                                       zT[:, h, blk * 512:(blk + 1) * 512], start=(h == 0), stop=(h == DC - 1))
                ins.then_inc(unit_ps, 1)

            pe.wait_ge(h1_ok, 1)
            t.matmul(pb[5][0:B, 16:16 + ND], h1[:, :], te2_sb, start=True, stop=True).then_inc(tl_ps, 1)
            pe.wait_ge(task_dve, 5)
            t.transpose(pb[5][0:ND, 32:32 + B], tl[:, 2, :], ident[0:B, 0:B]).then_inc(td_ps, 1)
            pe.wait_ge(tdb_ok, 1)
            pe.wait_ge(ld_task, 16)
            for b in range(B):
                ins = t.matmul(pb[4][:, TPB * b * E:TPB * (b + 1) * E].rearrange("p (i e) -> p i e", e=E), tdb[:, b, :],
                               aff_sb[:, :].unsqueeze(1).broadcast_to([ND, TPB, E]),
                               start=False, stop=(b == B - 1), skip_group_check=True)
            ins.then_inc(logit_ps, 1)
            unit(0)
            pe.wait_ge(chosen_ok, 1)
            for i in range(NT):
                ins = t.matmul(pb[6][0:E, 0:P], chosen[:, i, :], ones_bf[:, :], start=(i == 0), stop=(i == NT - 1))
            ins.then_inc(count_ps, 1)
            t.matmul(pb[7][:, :], tri[:, :], chosen[:, :, :].rearrange("p i e -> p (i e)"), start=True, stop=False, skip_group_check=True)
            for i in range(NT - 1):
                ins = t.matmul(pb[7][:, (i + 1) * E:].rearrange("p (i e) -> p i e", e=E), ones_bf[:, :],
                               chosen[:, i, :].unsqueeze(1).broadcast_to([P, NT - 1 - i, E]),
                               start=False, stop=(i == NT - 2), skip_group_check=True)
            ins.then_inc(rank_ps, 1)
            pe.wait_ge(halves_ok, 3)
            t.matmul(pb[5][:, 64:64 + E], halves_bf[:, :], tri[0:E, 0:E], start=True, stop=True)
            t.matmul(pb[5][0:E, 128:129], tri64i[:, :], halves_bf[:, 0:1], start=True, stop=True).then_inc(base_ps, 1)
            unit(1)
            unit(2)
            for j in range(NJ):
                pe.wait_ge(onehot, 3 * (j + 1))
                ins = t.matmul(pb[6][:, 128:128 + 2 * NPAIR], oh_lane[:, j % 4, :],
                               oh_tile[:, j % 4, :, :].rearrange("p a n -> p (a n)"), start=(j == 0), stop=(j == NJ - 1))
                ins.then_inc(listed, 1)
            pe.wait_ge(listed, NJ)
            pe.wait_ge(cmp_ok, 2)
            t.matmul(pb[5][0:1, 192:192 + E], ones_bf[0:E, 0:1], cmp[:, :], start=True, stop=True).then_inc(half_ps, 1)
            for n in range(3, EARLY):
                unit(n)
            pe.wait_ge(unit_sb, 2 * EARLY)

            for s in range(NPAIR + 3):
                if s < NPAIR:
                    pe.wait_ge(got[s % NG], 16 * (s // NG + 1))
                    if s >= 2:
                        pe.wait_ge(xT_sb, s - 1)
                    for h in range(DC):
                        ins = t.transpose(pb[s % 2][:, h * P:(h + 1) * P], xg[:, s % NG, h::DC], ident[:, :])
                    ins.then_inc(xT_ps, 1)
                if 1 <= s <= NPAIR:
                    q = s - 1
                    gu, _ = res(q)
                    if q < NMAIN:
                        pe.wait_ge(ld_gu[q // 4], 16)
                    else:
                        pe.wait_ge(ring_in[(q - NMAIN) % RING], 64 * ((q - NMAIN) // RING + 1))
                    pe.wait_ge(xT_sb, q + 1)
                    if q >= 2:
                        pe.wait_ge(h_ok, q - 1)
                    for a in range(2):
                        n = slice(a * HALF, (a + 1) * HALF)
                        for h in range(DC):
                            ins = t.matmul(pb[2 + q % 2][:, n], gu(a, h), xgT[:, q % 2, h, n], start=(h == 0), stop=(h == DC - 1))
                    ins.then_inc(gu_ps, 1)
                if s >= 3:
                    q = s - 3
                    _, wdq = res(q)
                    if q < NMAIN:
                        pe.wait_ge(ld_d[q // 8], 16)
                    pe.wait_ge(h_ok, q + 1)
                    if q >= 2:
                        pe.wait_ge(y_sb, q - 1)
                    t.matmul(pb[4 + q % 2][:, 0:D], hT[:, q % 2, :], wdq, start=True, stop=True).then_inc(y_ps, 1)
            for n in range(EARLY, UNITS):
                unit(n)
            pe.wait_ge(unit_h, EARLY)
            pe.wait_ge(unit_h_dve, UNITS - EARLY)
            pe.wait_ge(y_sb, NPAIR)
            for i in range(NT):
                if i >= 2:
                    pe.wait_ge(mixed, (i - 2) * (K + 1) + 1)
                for q in range(NSH * DC):
                    ins = t.matmul(pb[4 + i % 2][:, 0:D], hsh[:, q, i * P:(i + 1) * P], sd_sb[:, q, :],
                                   start=(q == 0), stop=(q == NSH * DC - 1))
                ins.then_inc(down_ps, 1)


def kernel(x, ctx_512, mask_SxS2_bk1, mask_BxS2_bf0, L0_xattn_Wq, L0_xattn_bq, L0_xattn_Wk, L0_xattn_bk,
           L0_ffn_Wr, L0_ffn_router_bias, L0_ffn_affinity, L0_ffn_te_W1, L0_ffn_te_b1, L0_ffn_te_W2,
           L0_ffn_te_b2, L0_ffn_Wg, L0_ffn_Wu, L0_ffn_Wd, L0_ffn_Sg, L0_ffn_Su, L0_ffn_Sd):
    import numpy as np
    import concourse.bacc as bacc
    from concourse.bass_utils import run_bass_kernel_spmd

    def by_feature(w):
        return w.reshape(P, DC, -1)

    sgu = np.stack([np.stack([by_feature(L0_ffn_Sg[i]), by_feature(L0_ffn_Su[i])], 1) for i in range(NSH)], 1)
    sd = L0_ffn_Sd.reshape(NSH * DC, P, D).transpose(1, 0, 2)
    arrays = {
        "x": x.reshape(N, D),
        "proj": np.concatenate([ctx_512.reshape(N, H).T, L0_xattn_Wq.T, L0_xattn_Wk.T,
                                L0_xattn_bq[:, None], L0_xattn_bk[:, None]], 1),
        "amask": mask_SxS2_bk1,
        "kmask": mask_BxS2_bf0.reshape(B * S),
        "router": np.concatenate([by_feature(L0_ffn_Wr.T).reshape(P, -1), by_feature(L0_ffn_te_W1.T).reshape(P, -1),
                                  L0_ffn_te_W2.T, L0_ffn_te_b1[:, None]], 1),
        "task": L0_ffn_affinity.T,
        "b2": L0_ffn_te_b2,
        "rbias": L0_ffn_router_bias,
        "shared": np.concatenate([sgu.reshape(P, -1), sd.reshape(P, -1)], 1),
        "wgu": np.stack([L0_ffn_Wg.reshape(E, P, DC, F), L0_ffn_Wu.reshape(E, P, DC, F)], 3).reshape(E, P, -1),
        "wd": L0_ffn_Wd,
    }
    arrays = {k: np.ascontiguousarray(v) for k, v in arrays.items()}
    nc = bacc.Bacc("TRN2", target_bir_lowering=False, num_devices=1)
    aps = {k: nc.dram_tensor(f"in_{k}", v.shape, mybir.dt.from_np(v.dtype), kind="ExternalInput").ap() for k, v in arrays.items()}
    out = nc.dram_tensor("out", (N, D), F32, kind="ExternalOutput").ap()
    build_xattn_moe(nc, *aps.values(), out)
    r = run_bass_kernel_spmd(nc, [{f"in_{k}": v for k, v in arrays.items()}], core_ids=[0])
    return r.results[0]["out"].reshape(B, S, D)
```

```python
from contextlib import ExitStack

import concourse.bass as bass
from concourse import mybir

F32 = mybir.dt.float32
F16 = mybir.dt.float16
BF16 = mybir.dt.bfloat16
I32 = mybir.dt.int32
U32 = mybir.dt.uint32
U8 = mybir.dt.uint8
ALU = mybir.AluOpType
ACT = mybir.ActivationFunctionType
AX = mybir.AxisListType

P = 128
B, S, D = 4, 256, 256
H = 64
E, F, K, ND = 64, 64, 4, 4
NSH, HSH = 2, 256
N = B * S
NT = N // P
TPB = S // P
DC = D // P
MAXT = 96
SLOTS = MAXT * P
NJ = NT * K
GJ = 2 * K
BIG = 1e30
SENTINEL = -3e38
CHOSEN = 3e38
ROUND = 12582912.0
SKIP = 5001.0
EPS = 1e-5

U = 8
FILL_TURNS = 3
FILL_TILE = N * K // P + FILL_TURNS * U
YB = 4
GU_LAG, D_LAG = 1, 4
NC = 8
UNITS = NSH * DC * 2


def build_xattn_moe(nc, x, proj, amask, kmask, router, task, b2, rbias, shared, wgu, wd, out):
    z_dram = nc.dram_tensor("z_rows", (N, D), F32, kind="Internal").ap()
    y_dram = nc.dram_tensor("y_slots", (SLOTS, D), F32, kind="Internal").ap()

    with ExitStack() as ctx:
        def sb(name, shape, dt=F32):
            return ctx.enter_context(nc.sbuf_tensor(name, shape, dt))

        def sem(name):
            return ctx.enter_context(nc.semaphore(name))

        wgu_sb = sb("wgu_sb", [P, E, DC, 2 * F])
        wd_sb = sb("wd_sb", [P, E // 2, D])
        shared_sb = sb("shared_sb", [P, NSH * 2 * DC * HSH + NSH * DC * D])
        sgu_sb = shared_sb[:, 0:NSH * 2 * DC * HSH].rearrange("p (i g c h) -> p i g c h", i=NSH, g=2, c=DC)
        sd_sb = shared_sb[:, NSH * 2 * DC * HSH:].rearrange("p (q d) -> p q d", d=D)
        proj_sb = sb("proj_sb", [P, N + 2 * H + 2])
        router_sb = sb("router_sb", [P, DC * E + DC * P + ND + 1])
        wr_sb = router_sb[:, 0:DC * E].rearrange("p (c e) -> p c e", c=DC)
        te1_sb = router_sb[:, DC * E:DC * (E + P)].rearrange("p (c j) -> p c j", c=DC)
        te2_sb = router_sb[:, DC * (E + P):DC * (E + P) + ND]
        b1_sb = router_sb[:, DC * (E + P) + ND:]
        aff_sb = sb("aff_sb", [ND, E])
        b2_sb = sb("b2_sb", [B, ND])
        rb_sb = sb("rb_sb", [P, E])
        amask_sb = sb("amask_sb", [P, TPB, S], U8)
        kmask_sb = sb("kmask_sb", [P, B * S], U8)

        xs = sb("xs", [P, NT, D])
        z = sb("z", [P, NT, D])
        zT = sb("zT", [P, DC, N])
        hsh = sb("hsh", [P, NSH * DC, N])
        qc = hsh[:, 0:2, :].rearrange("p a n -> p (a n)").rearrange("p (i d) -> p i d", d=D)
        mb = hsh[:, 2:4, :].rearrange("p a (b s) -> p a b s", b=B)
        qkT = sb("qkT", [P, 2, N])
        sgu_v = qkT[:, :, :].rearrange("p a (r n) -> p a r n", r=2)
        sc = sb("sc", [P, 2, TPB, S])
        kneg = z[:, 0:B, :].rearrange("p b t -> p (b t)")
        aneg = z[:, B:B + TPB, :]
        xg = sb("xg", [P, U, D])
        xgT = sb("xgT", [P, 2, DC, P])
        sg = sb("sg", [P, 2, F])
        hh = sb("hh", [P, 2, 2, F])
        hT = sb("hT", [P, 2, P])
        ysb = sb("ysb", [P, YB, D])
        zero_row = sb("zero_row", [P, D])
        tok_now = sb("tok_now", [P, U], U32)

        ident = sb("ident", [P, P])
        ones_bf = sb("ones_bf", [P, P], BF16)
        tri = sb("tri", [P, P], BF16)
        tri_less = sb("tri_less", [E, E], BF16)
        lanes = sb("lanes", [P, P, GJ], F16)
        tok_no = sb("tok_no", [P, NT])

        st = sb("st", [P, NT, 6])
        mv1 = sb("mv1", [P, NT, 2])
        mv2 = sb("mv2", [P, NT, 2])
        rstd1 = sb("rstd1", [P, NT])
        rstd2 = sb("rstd2", [P, NT])
        nmr1 = sb("nmr1", [P, NT])
        nmr2 = sb("nmr2", [P, NT])
        veps = sb("veps", [P, 2, NT])
        mhalf = sb("mhalf", [P, NT])
        smax = sb("smax", [P, NT])
        nmax = sb("nmax", [P, NT])
        ssum = sb("ssum", [P, NT])
        skeep = sb("skeep", [P, NT])
        rinv = sb("rinv", [P, NT])
        zsum = sb("zsum", [P, DC, B])
        h1 = sb("h1", [P, B])
        tl = sb("tl", [B, 4, ND])
        ts_ = sb("ts_", [B, 4])
        tdT = sb("tdT", [ND, B])
        lb = proj_sb[:, 0:NT * (E + 4)].rearrange("p (i e) -> p i e", i=NT)
        marked = proj_sb[:, NT * (E + 4):2 * NT * (E + 4)].rearrange("p (i e) -> p i e", i=NT)
        top8 = sb("top8", [P, NT, 8])
        chosen = sb("chosen", [P, NT, E], BF16)
        logit = sb("logit", [P, NT, E])
        lmax = sb("lmax", [P, NT])
        slotmap = sb("slotmap", [P, NT, E])
        need = sb("need", [E, 2, P])
        need_bf = sb("need_bf", [E, P], BF16)
        slot8 = sb("slot8", [P, NT, 8])
        slot_i = sb("slot_i", [P, 3, NJ], I32)
        slot_h = sb("slot_h", [P, 2, NJ], F16)
        oh_lane = (sc[:, :, :, :].rearrange("p a c s -> p (a c s)").bitcast(F16)
                   .rearrange("p (n l j) -> p n l j", n=2, j=GJ))
        oh_tile = sb("oh_tile", [P, 2, MAXT, GJ], F16)
        oh_val = sb("oh_val", [P, 2, MAXT, GJ], F16)
        empty = sb("empty", [P, MAXT])
        tok = sb("tok", [P, MAXT + U], U32)
        cuml = sb("cuml", [E, 1])
        cmp = sb("cmp", [E, MAXT], BF16)
        tile_e = sb("tile_e", [P, 2, MAXT], I32)
        gu_at = sb("gu_at", [1, MAXT + U], I32)
        d_at = sb("d_at", [1, MAXT + U], I32)
        parity = sb("parity", [P, 2, MAXT])
        turns = sb("turns", [1, 3], I32)
        pick = sb("pick", [P, NJ])
        junk = sc[:, 1, :, :].rearrange("p c s -> p (c s)").rearrange("p (n e) -> p n e", e=E)
        zden = sb("zden", [P, 3, NT])
        wgt = sb("wgt", [P, NJ])

        pb = [ctx.enter_context(nc.psum_tensor(f"pb{i}", [P, 512], F32)) for i in range(8)]

        ld_proj, ld_mask, ld_router = sem("ld_proj"), sem("ld_mask"), sem("ld_router")
        ld_task, ld_b2, ld_rb, ld_shared, ld_kmask = sem("ld_task"), sem("ld_b2"), sem("ld_rb"), sem("ld_shared"), sem("ld_kmask")
        ld_x = [sem(f"ld_x{b}") for b in range(B)]
        ld_gu = [sem(f"ld_gu{n}") for n in range(8)]
        ld_d = [sem(f"ld_d{n}") for n in range(4)]
        const_ok, aneg_ok, mask_ok = sem("const_ok"), sem("aneg_ok"), sem("mask_ok")
        proj_ps, qk_sb = sem("proj_ps"), sem("qk_sb")
        stat1, mv1_ok, var1, rstd1_ok, nmr1_ok, qc_ok = sem("stat1"), sem("mv1_ok"), sem("var1"), sem("rstd1_ok"), sem("nmr1_ok"), sem("qc_ok")
        score_ps, score_x, score_m, nmax_ok, exp_ok = (sem("score_ps"), sem("score_x"), sem("score_m"), sem("nmax_ok"), sem("exp_ok"))
        keep_ok, rinv_ok, x1_ok = sem("keep_ok"), sem("rinv_ok"), sem("x1_ok")
        stat2, mv2_ok, var2, rstd2_ok, nmr2_ok, z_ok = (
            sem("stat2"), sem("mv2_ok"), sem("var2"), sem("rstd2_ok"), sem("nmr2_ok"), sem("z_ok"))
        z_out = sem("z_out")
        zT_ps, zT_sb = sem("zT_ps"), sem("zT_sb")
        h1_ps, h1_ok, tl_ps, task_dve, task_exp, td_ps, tdT_ok = (
            sem("h1_ps"), sem("h1_ok"), sem("tl_ps"), sem("task_dve"), sem("task_exp"), sem("td_ps"), sem("tdT_ok"))
        logit_ps, lb_ok, top_ok, cut_ok, marked_ok, chosen_ok = (
            sem("logit_ps"), sem("lb_ok"), sem("top_ok"), sem("cut_ok"), sem("marked_ok"), sem("chosen_ok"))
        count_ps, need_ok, rank_ps, slot_ok = sem("count_ps"), sem("need_ok"), sem("rank_ps"), sem("slot_ok")
        slot8_ok, slotf, onehot, valued, listed, tok_step = (
            sem("slot8_ok"), sem("slotf"), sem("onehot"), sem("valued"), sem("listed"), sem("tok_step"))
        cmp_ok, turns_step, expert_ps, expert_step, at_ok = sem("cmp_ok"), sem("turns_step"), sem("expert_ps"), sem("expert_step"), sem("at_ok")
        logit_sb, lmax_ok, lsub_ok, lexp_ok = sem("logit_sb"), sem("lmax_ok"), sem("lsub_ok"), sem("lexp_ok")
        unit_ps, unit_sb, unit_h, unit_v = sem("unit_ps"), sem("unit_sb"), sem("unit_h"), sem("unit_v")
        got = [sem(f"got{n}") for n in range(U)]
        xT_ps, xT_sb, tok_set, gu_ps, silu_ok, h_ok, hT_ps, hT_sb, y_ps, y_sb = (
            sem("xT_ps"), sem("xT_sb"), sem("tok_set"), sem("gu_ps"), sem("silu_ok"), sem("h_ok"), sem("hT_ps"),
            sem("hT_sb"), sem("y_ps"), sem("y_sb"))
        zeroed, y_fill = sem("zeroed"), sem("y_fill")
        y_out = [sem(f"y_out{n}") for n in range(YB)]
        back = [sem(f"back{n}") for n in range(NC)]
        pick_ok, w_step = sem("pick_ok"), sem("w_step")
        down_ps, mixed, out_ok = sem("down_ps"), sem("mixed"), sem("out_ok")

        def x_rows(dram, b):
            return dram[b * S:(b + 1) * S, :].rearrange("(c p) d -> p c d", p=P)

        def turn_count(eng):
            eng.wait_ge(turns_step, 3)
            return eng.value_load(turns[0:1, 1:2], min_val=N * K // P // U, max_val=MAXT // U)

        def last_turn_end(eng):
            return eng.value_load(turns[0:1, 2:3], min_val=N * K // P - 2 * U, max_val=MAXT - 2 * U) + 2 * U

        def unit_of(n):
            return (0, n // 2, n % 2) if n < 4 else (1, n % 2, n // 2 - 2)

        block = ctx.enter_context(nc.Block())

        def over_tiles(eng, stages, lags):
            for k in range(U):
                stages(0, k, lambda lag: k >= lag)
            n_turns = turn_count(eng)
            with eng.Fori(1, 2) as turn:
                for k in range(U):
                    stages(turn * U, k, lambda lag: U + k >= lag)
            with eng.Fori(2, n_turns) as turn:
                for k in range(U):
                    stages(turn * U, k, lambda lag: True)
            end = last_turn_end(eng)
            for k in range(lags - 1):
                stages(end, k, lambda lag: k < lag)
            return end

        @block.sync
        def _(sp):
            sp.dma_start(proj_sb[0:H, :], proj).then_inc(ld_proj, 16)
            sp.dma_start(xs[:, 0:TPB, :], x_rows(x, 0)).then_inc(ld_x[0], 16)
            sp.dma_start(kmask_sb[:, :], kmask.partition_broadcast(P)).then_inc(ld_kmask, 16)
            sp.dma_start(amask_sb[:, :, :], amask.rearrange("(c p) t -> p c t", p=P)).then_inc(ld_mask, 16)
            for b in range(1, B):
                sp.dma_start(xs[:, TPB * b:TPB * (b + 1), :], x_rows(x, b)).then_inc(ld_x[b], 16)
            sp.dma_start(router_sb[:, :], router).then_inc(ld_router, 16)
            sp.dma_start(aff_sb[:, :], task).then_inc(ld_task, 16)
            sp.dma_start(b2_sb[:, :], b2.partition_broadcast(B)).then_inc(ld_b2, 16)
            sp.dma_start(rb_sb[:, :], rbias.partition_broadcast(P)).then_inc(ld_rb, 16)
            sp.dma_start(shared_sb[:, :], shared).then_inc(ld_shared, 16)
            def load_weights(n):
                sp.dma_start(wgu_sb[:, 8 * n:8 * (n + 1), :, :].rearrange("p e c f -> p e (c f)"),
                             wgu[8 * n:8 * (n + 1), :, :].rearrange("e p n -> p e n")).then_inc(ld_gu[n], 16)
                if n % 2 == 0:
                    q = 4 * n
                    sp.dma_start(wd_sb[:, q:q + 8, :],
                                 wd[2 * q:2 * q + 16, :, :].rearrange("(q a) f d -> (a f) q d", a=2)).then_inc(ld_d[n // 2], 16)
            for n in range(4):
                load_weights(n)
            for b in range(B):
                sp.wait_ge(z_ok, TPB * (b + 1))
                sp.dma_start(x_rows(z_dram, b), z[:, TPB * b:TPB * (b + 1), :]).then_inc(z_out, 16)
                load_weights(4 + b)
            sp.wait_ge(zeroed, 2)
            for t in range(FILL_TILE, MAXT, U):
                sp.dma_start(y_dram[t * P:(t + U) * P, :].rearrange("(u p) d -> p u d", p=P),
                             zero_row[:, :].unsqueeze(1).broadcast_to([P, U, D])).then_inc(y_fill, 16)
            n_turns = turn_count(sp)
            def store(first, k):
                sp.wait_ge(y_sb, first + k + 1)
                sp.dma_start(y_dram[bass.ds((first + k) * P, P), :], ysb[:, k % YB, :]).then_inc(y_out[k % YB], 16)

            def store_and_fill(first, k):
                sp.dma_start(y_dram[bass.ds((first + k + N * K // P) * P, P), :], zero_row[:, :]).then_inc(y_fill, 16)
                store(first, k)

            for k in range(U):
                store_and_fill(0, k)
            with sp.Fori(1, FILL_TURNS) as turn:
                for k in range(U):
                    store_and_fill(turn * U, k)
            sp.wait_ge(y_fill, 16 * ((MAXT - FILL_TILE) // U + FILL_TURNS * U))
            with sp.Fori(FILL_TURNS, n_turns) as turn:
                for k in range(U):
                    store(turn * U, k)
            for i in range(NT):
                sp.wait_ge(mixed, (i + 1) * (K + 1))
                sp.dma_start(out[i * P:(i + 1) * P, :], xs[:, i, :]).then_inc(out_ok, 16)
            sp.wait_ge(out_ok, 16 * NT)

        @block.gpsimd
        def _(pool):
            g = nc.gpsimd
            g.memset(mhalf[:, :], -0.5).then_inc(const_ok, 1)
            g.memset(ident[:, :], 0.0).then_inc(const_ok, 1)
            g.memset(ones_bf[:, :], 1.0).then_inc(const_ok, 1)
            g.iota(lanes[:, :, :], [[1, P], [0, GJ]], base=0, channel_multiplier=0, allow_small_or_imprecise_dtypes=True).then_inc(const_ok, 1)
            g.iota(tok_no[:, :], [[P, NT]], base=1, channel_multiplier=1, allow_small_or_imprecise_dtypes=True).then_inc(const_ok, 1)
            pool.wait_ge(const_ok, 3)
            g.affine_select(out=ident[:, :], in_=ident[:, :], compare_op=ALU.not_equal, fill=1.0, base=0,
                            pattern=[[-1, P]], channel_multiplier=1).then_inc(const_ok, 1)
            g.affine_select(out=tri[:, :], in_=ones_bf[:, :], compare_op=ALU.is_ge, fill=0.0, base=0,
                            pattern=[[1, P]], channel_multiplier=-1).then_inc(const_ok, 1)
            g.memset(tri_less[:, :], float(P)).then_inc(const_ok, 1)
            pool.wait_ge(const_ok, 8)
            g.affine_select(out=tri_less[:, :], in_=tri_less[:, :], compare_op=ALU.is_gt, fill=0.0, base=0,
                            pattern=[[1, E]], channel_multiplier=-1).then_inc(const_ok, 1)

            for b in range(B):
                t = slice(TPB * b, TPB * (b + 1))
                pool.wait_ge(var1, b + 1)
                g.tensor_tensor(rstd1[:, t], veps[:, 0, t], mhalf[:, t], ALU.pow).then_inc(rstd1_ok, 1)
                if b == 0:
                    pool.wait_ge(ld_mask, 16)
                    g.tensor_scalar(aneg, amask_sb[:, :, :], -BIG, None, ALU.mult).then_inc(aneg_ok, 1)
                    pool.wait_ge(aneg_ok, 1)
                    pool.wait_ge(mask_ok, 1)
                g.tensor_tensor(mb[:, :, b, :], aneg, kneg[:, b * S:(b + 1) * S].unsqueeze(1).broadcast_to([P, TPB, S]),
                                ALU.add).then_inc(mask_ok, 1)
            for b in range(B):
                pool.wait_ge(var2, b + 1)
                t = slice(TPB * b, TPB * (b + 1))
                g.tensor_tensor(rstd2[:, t], veps[:, 1, t], mhalf[:, t], ALU.pow).then_inc(rstd2_ok, 1)

            pool.wait_ge(lmax_ok, 1)
            g.tensor_tensor(logit[:, :, :], logit[:, :, :], lmax[:, :].unsqueeze(2).broadcast_to([P, NT, E]),
                            ALU.subtract).then_inc(lsub_ok, 1)

            for n in range(2):
                i, hc, blk = unit_of(n)
                pool.wait_ge(unit_sb, 2 * n + 2)
                g.tensor_tensor(hsh[:, 2 * i + hc, blk * 512:(blk + 1) * 512], sgu_v[:, 0, n % 2, :], sgu_v[:, 1, n % 2, :],
                                ALU.mult).then_inc(unit_h, 1)

            pool.wait_ge(z_out, 16 * B)
            pool.wait_ge(zeroed, 1)

            tile_no = ctx.enter_context(pool.register("tile_no"))
            pool.reg_mov(tile_no, 1)

            def gather(k):
                pool.wait_ge(tok_set, tile_no)
                pool.reg_add(tile_no, tile_no, 1)
                g.indirect_dma_start(xg[:, k, :], None, z_dram, bass.IndirectOffsetOnAxis(ap=tok_now[:, k:k + 1], axis=0),
                                     bounds_check=N - 1, oob_is_err=False).then_inc(got[k], 16)

            for k in range(U):
                gather(k)
            n_turns = turn_count(pool)
            with pool.Fori(1, n_turns) as _:
                for k in range(U):
                    gather(k)
            for n in range(YB):
                pool.wait_ge(y_out[n], n_turns * (16 * U // YB))
            last_row = n_turns * (U * P) - 1
            for j in range(NJ):
                if j >= NC:
                    i = (j - NC) // K
                    pool.wait_ge(mixed, i * (K + 1) + (j - NC) % K + 1)
                g.indirect_dma_start(z[:, j % NC, :], None, y_dram,
                                     bass.IndirectOffsetOnAxis(ap=slot_i[:, 0, j:j + 1].bitcast(U32), axis=0),
                                     bounds_check=last_row, oob_is_err=False).then_inc(back[j % NC], 16)

        def evac_zT(act, b):
            act.wait_ge(zT_ps, b + 1)
            for c in range(DC):
                nc.scalar.activation(zT[:, c, b * S:(b + 1) * S], pb[b][:, c * S:(c + 1) * S], ACT.Identity,
                                     accum_out=zsum[:, c, b:b + 1]).then_inc(zT_sb, 1)

        @block.scalar
        def _(act):
            a = nc.scalar
            for blk in range(2):
                act.wait_ge(proj_ps, blk + 1)
                for w in range(2):
                    a.activation(qkT[0:H, w, blk * 512:(blk + 1) * 512], pb[blk][w * H:(w + 1) * H, :], ACT.Identity,
                                 bias=proj_sb[0:H, N + 2 * H + w:N + 2 * H + w + 1]).then_inc(qk_sb, 1)
            for i in range(NT):
                act.wait_ge(nmr1_ok, i // TPB + 1)
                a.activation(qc[:, i, :], xs[:, i, :], ACT.Identity, bias=nmr1[:, i:i + 1], scale=rstd1[:, i:i + 1]).then_inc(qc_ok, 1)

            def normalise(b):
                act.wait_ge(nmr2_ok, b + 1)
                for c in range(TPB):
                    i = TPB * b + c
                    a.activation(z[:, i, :], xs[:, i, :], ACT.Identity, bias=nmr2[:, i:i + 1], scale=rstd2[:, i:i + 1]).then_inc(z_ok, 1)

            for b in range(B):
                for c in range(TPB):
                    i = TPB * b + c
                    act.wait_ge(nmax_ok, b + 1)
                    a.activation(sc[:, b % 2, c, :], sc[:, b % 2, c, :], ACT.Exp, bias=nmax[:, i:i + 1],
                                 accum_out=ssum[:, i:i + 1]).then_inc(exp_ok, 1)
                if b >= 1:
                    normalise(b - 1)
                if b >= 2:
                    evac_zT(act, b - 2)
            normalise(B - 1)
            evac_zT(act, B - 2)
            evac_zT(act, B - 1)
            act.wait_ge(h1_ps, 1)
            a.activation(h1[:, :], pb[5][:, 0:B], ACT.Gelu, bias=b1_sb, scale=1.0 / S).then_inc(h1_ok, 1)
            act.wait_ge(task_dve, 3)
            a.activation(tl[:, 1, :], tl[:, 0, :], ACT.Exp, bias=ts_[:, 1:2], accum_out=ts_[:, 2:3]).then_inc(task_exp, 1)
            act.wait_ge(lb_ok, 2)
            a.activation(logit[:, :, :], pb[4][:, :].rearrange("p (i e) -> p i e", e=E), ACT.Identity).then_inc(logit_sb, 1)
            act.wait_ge(lsub_ok, 1)
            a.activation(logit[:, :, :], logit[:, :, :], ACT.Exp).then_inc(lexp_ok, 1)

            def unit(n):
                act.wait_ge(unit_ps, n + 1)
                if 2 <= n < 4:
                    act.wait_ge(unit_h, n - 1)
                elif n >= 4:
                    act.wait_ge(unit_v, n - 3)
                bank = 2 * (n % 2)
                a.activation(sgu_v[:, 0, n % 2, :], pb[bank][:, :], ACT.Silu).then_inc(unit_sb, 1)
                if n < 4:
                    a.activation(sgu_v[:, 1, n % 2, :], pb[bank + 1][:, :], ACT.Identity).then_inc(unit_sb, 1)

            def value(r):
                n = r % 2
                act.wait_ge(onehot, 2 * r + 1)
                if r >= 2:
                    act.wait_ge(listed, r - 1)
                for c in range(GJ // K):
                    i = r * GJ // K + c
                    a.activation(oh_val[:, n, :, c * K:(c + 1) * K], oh_tile[:, n, :, c * K:(c + 1) * K], ACT.Identity,
                                 scale=tok_no[:, i:i + 1]).then_inc(valued, 1)

            unit(0)
            unit(1)
            for r in range(NJ // GJ):
                value(r)
            unit(2)
            unit(3)

            def stages(first, k, have):
                if have(5):
                    q, n = first + (k - 5), (k - 5) % YB
                    act.wait_ge(y_ps, q + 1)
                    if have(5 + YB):
                        act.wait_ge(y_out[n], (first + (k - 5 - n)) * (16 // YB))
                    a.activation(ysb[:, n, :], pb[4 + n % 2][:, 0:D], ACT.Identity).then_inc(y_sb, 1)
                if have(1):
                    q, n = first + (k - 1), (k - 1) % 2
                    act.wait_ge(gu_ps, q + 1)
                    if have(3):
                        act.wait_ge(h_ok, q - 1)
                    a.activation(sg[:, n, :], pb[2 + n][:, 0:F], ACT.Silu).then_inc(silu_ok, 1)
                if have(3):
                    q, n = first + (k - 3), (k - 3) % 2
                    act.wait_ge(hT_ps, q + 1)
                    if have(5):
                        act.wait_ge(y_ps, q - 1)
                    a.activation(hT[:, n, :], pb[6][:, 0:P], ACT.Identity).then_inc(hT_sb, 1)

            over_tiles(act, stages, 6)
            for n in range(4, UNITS):
                unit(n)

        @block.vector
        def _(dve):
            v = nc.vector
            v.memset(xg[:, :, :], 0.0).then_inc(zeroed, 1)
            v.memset(zero_row[:, :], 0.0).then_inc(zeroed, 1)
            v.memset(gu_at[:, :], 0).then_inc(at_ok, 1)
            v.memset(d_at[:, :], 0).then_inc(at_ok, 1)
            v.memset(tok[:, MAXT:], 0).then_inc(tok_step, 1)

            def stats(b):
                t = slice(TPB * b, TPB * (b + 1))
                dve.wait_ge(ld_x[b], 16)
                for i in range(TPB * b, TPB * (b + 1)):
                    v.bn_stats(st[:, i, :], xs[:, i, :]).then_inc(stat1, 1)
                for i in range(TPB * b, TPB * (b + 1)):
                    dve.wait_ge(stat1, i + 1)
                    v.bn_aggr(mv1[:, i, :], st[:, i, :]).then_inc(mv1_ok, 1)
                dve.wait_ge(mv1_ok, TPB * (b + 1))
                v.tensor_scalar(veps[:, 0, t], mv1[:, t, 1], EPS, None, ALU.add).then_inc(var1, 1)

            def shift1(b):
                t = slice(TPB * b, TPB * (b + 1))
                dve.wait_ge(rstd1_ok, b + 1)
                v.scalar_tensor_tensor(nmr1[:, t], mv1[:, t, 0], -1.0, rstd1[:, t], ALU.mult, ALU.mult).then_inc(nmr1_ok, 1)

            def scores(b):
                sl = sc[:, b % 2, :, :]
                dve.wait_ge(score_ps, b + 1)
                dve.wait_ge(qc_ok, TPB * (b + 1))
                if b >= 2:
                    dve.wait_ge(x1_ok, TPB * (b - 1))
                v.scalar_tensor_tensor(sl, pb[4 + b][:, :].rearrange("p (c t) -> p c t", c=TPB), float(H) ** -0.5,
                                       qc[:, TPB * b:TPB * (b + 1), :], ALU.mult, ALU.mult).then_inc(score_x, 1)
                dve.wait_ge(score_x, b + 1)
                dve.wait_ge(mask_ok, 2 + b)
                for c in range(TPB):
                    i = TPB * b + c
                    v.tensor_tensor_reduce(sc[:, b % 2, c, :], sc[:, b % 2, c, :], mb[:, c, b, :], 1.0, SENTINEL,
                                           ALU.add, ALU.max, smax[:, i:i + 1]).then_inc(score_m, 1)
                t = slice(TPB * b, TPB * (b + 1))
                dve.wait_ge(score_m, TPB * (b + 1))
                v.tensor_scalar(nmax[:, t], smax[:, t], -1.0, None, ALU.mult).then_inc(nmax_ok, 1)

            def finish(b):
                t = slice(TPB * b, TPB * (b + 1))
                dve.wait_ge(exp_ok, TPB * (b + 1))
                v.scalar_tensor_tensor(skeep[:, t], smax[:, t], -0.5 * BIG, ssum[:, t], ALU.is_gt, ALU.mult).then_inc(keep_ok, 1)
                dve.wait_ge(keep_ok, b + 1)
                v.reciprocal(rinv[:, t], skeep[:, t]).then_inc(rinv_ok, 1)
                dve.wait_ge(rinv_ok, b + 1)
                for c in range(TPB):
                    i = TPB * b + c
                    v.scalar_tensor_tensor(xs[:, i, :], sc[:, b % 2, c, :], rinv[:, i:i + 1], xs[:, i, :],
                                           ALU.mult, ALU.add).then_inc(x1_ok, 1)
                for c in range(TPB):
                    i = TPB * b + c
                    dve.wait_ge(x1_ok, i + 1)
                    v.bn_stats(st[:, i, :], xs[:, i, :]).then_inc(stat2, 1)
                for c in range(TPB):
                    i = TPB * b + c
                    dve.wait_ge(stat2, i + 1)
                    v.bn_aggr(mv2[:, i, :], st[:, i, :]).then_inc(mv2_ok, 1)
                dve.wait_ge(mv2_ok, TPB * (b + 1))
                v.tensor_scalar(veps[:, 1, t], mv2[:, t, 1], EPS, None, ALU.add).then_inc(var2, 1)

            def shift2(b):
                t = slice(TPB * b, TPB * (b + 1))
                dve.wait_ge(rstd2_ok, b + 1)
                v.scalar_tensor_tensor(nmr2[:, t], mv2[:, t, 0], -1.0, rstd2[:, t], ALU.mult, ALU.mult).then_inc(nmr2_ok, 1)

            stats(0)
            dve.wait_ge(ld_kmask, 16)
            v.tensor_scalar(kneg[:, :], kmask_sb[:, :], -BIG, None, ALU.mult).then_inc(mask_ok, 1)
            stats(1)
            shift1(0)
            stats(2)
            shift1(1)
            scores(0)
            stats(3)
            shift1(2)
            scores(1)
            shift1(3)
            finish(0)
            for b in range(2, B):
                scores(b)
                if b == 2:
                    dve.wait_ge(mask_ok, 1 + B)
                shift2(b - 2)
                finish(b - 1)
            shift2(B - 2)
            finish(B - 1)
            shift2(B - 1)

            v.memset(lb[:, :, E:E + 4], SENTINEL).then_inc(lb_ok, 1)
            dve.wait_ge(tl_ps, 1)
            dve.wait_ge(ld_b2, 16)
            v.tensor_tensor(tl[:, 0, :], pb[5][0:B, 16:16 + ND], b2_sb[:, :], ALU.add).then_inc(task_dve, 1)
            dve.wait_ge(task_dve, 1)
            v.tensor_reduce(ts_[:, 0:1], tl[:, 0, :], AX.X, ALU.max).then_inc(task_dve, 1)
            dve.wait_ge(task_dve, 2)
            v.tensor_scalar(ts_[:, 1:2], ts_[:, 0:1], -1.0, None, ALU.mult).then_inc(task_dve, 1)
            dve.wait_ge(task_exp, 1)
            v.reciprocal(ts_[:, 3:4], ts_[:, 2:3]).then_inc(task_dve, 1)
            dve.wait_ge(task_dve, 4)
            v.tensor_scalar(tl[:, 2, :], tl[:, 1, :], ts_[:, 3:4], 0.5, ALU.mult, ALU.mult).then_inc(task_dve, 1)
            dve.wait_ge(td_ps, 1)
            v.tensor_copy(tdT[:, :], pb[5][0:ND, 32:32 + B]).then_inc(tdT_ok, 1)

            dve.wait_ge(logit_ps, 1)
            dve.wait_ge(ld_rb, 16)
            lg = pb[4][:, :].rearrange("p (i e) -> p i e", e=E)
            v.tensor_tensor(lb[:, :, 0:E], lg, rb_sb[:, :].unsqueeze(1).broadcast_to([P, NT, E]), ALU.add).then_inc(lb_ok, 1)
            dve.wait_ge(lb_ok, 2)
            for i in range(NT):
                v.max(top8[:, i, :], lb[:, i, :]).then_inc(top_ok, 1)
            dve.wait_ge(top_ok, NT)
            v.memset(top8[:, :, K:8], SENTINEL).then_inc(cut_ok, 1)
            dve.wait_ge(cut_ok, 1)
            for i in range(NT):
                v.match_replace(marked[:, i, :], top8[:, i, :], lb[:, i, :], CHOSEN).then_inc(marked_ok, 1)
            dve.wait_ge(marked_ok, NT)
            v.tensor_scalar(chosen[:, :, :], marked[:, :, 0:E], CHOSEN, None, ALU.is_ge).then_inc(chosen_ok, 1)

            dve.wait_ge(logit_sb, 1)
            v.tensor_reduce(lmax[:, :], logit[:, :, :], AX.X, ALU.max).then_inc(lmax_ok, 1)
            dve.wait_ge(count_ps, 1)
            v.tensor_scalar(need[:, 0, :], pb[6][0:E, 0:P], 1.0 / P, 0.5 - 0.5 / P, ALU.mult, ALU.add).then_inc(need_ok, 1)
            dve.wait_ge(need_ok, 1)
            v.tensor_scalar(need_bf[:, :], need[:, 0, :], ROUND, -ROUND, ALU.add, ALU.add).then_inc(need_ok, 1)
            dve.wait_ge(rank_ps, 1)
            v.tensor_tensor(slotmap[:, :, :], pb[7][:, :].rearrange("p (i e) -> p i e", e=E), chosen[:, :, :], ALU.mult).then_inc(slot_ok, 1)
            dve.wait_ge(slot_ok, 1)
            for i in range(NT):
                v.max(slot8[:, i, :], slotmap[:, i, :]).then_inc(slot8_ok, 1)
            dve.wait_ge(slot8_ok, NT)
            v.tensor_scalar(slot_i[:, 0, :].rearrange("p (i k) -> p i k", k=K), slot8[:, :, 0:K], -1.0, None, ALU.add).then_inc(slotf, 1)
            dve.wait_ge(slotf, 1)
            v.tensor_scalar(slot_i[:, 1, :], slot_i[:, 0, :], P - 1, None, ALU.bitwise_and).then_inc(slotf, 1)
            v.tensor_scalar(slot_i[:, 2, :], slot_i[:, 0, :], 7, None, ALU.logical_shift_right).then_inc(slotf, 1)
            dve.wait_ge(slotf, 3)
            v.tensor_copy(slot_h[:, :, :], slot_i[:, 1:3, :]).then_inc(slotf, 1)
            dve.wait_ge(slotf, 4)
            for r in range(NJ // GJ):
                n, cols = r % 2, slice(r * GJ, (r + 1) * GJ)
                if r >= 2:
                    dve.wait_ge(listed, r - 1)
                    dve.wait_ge(valued, 2 * (r - 1))
                v.tensor_tensor(oh_tile[:, n, :, :], lanes[:, 0:MAXT, :],
                                slot_h[:, 1, cols].unsqueeze(1).broadcast_to([P, MAXT, GJ]), ALU.is_equal).then_inc(onehot, 1)
                v.tensor_tensor(oh_lane[:, n, :, :], lanes[:, :, :],
                                slot_h[:, 0, cols].unsqueeze(1).broadcast_to([P, P, GJ]), ALU.is_equal).then_inc(onehot, 1)
            dve.wait_ge(listed, NJ // GJ)
            v.tensor_scalar(empty[:, :], pb[6][:, 128:128 + MAXT], 0.0, SKIP, ALU.is_equal, ALU.mult).then_inc(tok_step, 1)
            dve.wait_ge(tok_step, 2)
            v.scalar_tensor_tensor(tok[:, 0:MAXT], pb[6][:, 128:128 + MAXT], -1.0, empty[:, :], ALU.add, ALU.add).then_inc(tok_step, 1)
            dve.wait_ge(tok_step, 3)
            for k in range(U):
                v.tensor_copy(tok_now[:, k:k + 1], tok[:, k:k + 1]).then_inc(tok_set, 1)
            dve.wait_ge(rank_ps, 2)
            v.tensor_copy(cuml[:, :], pb[5][0:E, 128:129]).then_inc(cmp_ok, 1)
            v.tensor_scalar(turns[:, 0:1], pb[5][0:1, 160:161], float(U - 1), None, ALU.add).then_inc(turns_step, 1)
            dve.wait_ge(turns_step, 1)
            v.tensor_scalar(turns[:, 1:2], turns[:, 0:1], U.bit_length() - 1, None, ALU.logical_shift_right).then_inc(turns_step, 1)
            dve.wait_ge(turns_step, 2)
            v.tensor_scalar(turns[:, 2:3], turns[:, 1:2], -2.0, float(U), ALU.add, ALU.mult).then_inc(turns_step, 1)
            dve.wait_ge(cmp_ok, 1)
            v.tensor_scalar(cmp[:, :], lanes[0:E, 0:MAXT, 0], cuml[:, :], None, ALU.is_ge).then_inc(cmp_ok, 1)
            dve.wait_ge(expert_ps, 1)
            v.tensor_scalar(tile_e[:, 0, :], pb[5][:, 192:192 + MAXT], float(E - 1), None, ALU.min).then_inc(expert_step, 1)
            dve.wait_ge(expert_step, 1)
            dve.wait_ge(at_ok, 2)
            v.tensor_copy(gu_at[:, GU_LAG:GU_LAG + MAXT], tile_e[0:1, 0, :]).then_inc(at_ok, 1)
            v.tensor_scalar(d_at[:, D_LAG:D_LAG + MAXT], tile_e[0:1, 0, :], 1, None, ALU.logical_shift_right).then_inc(at_ok, 1)
            v.tensor_scalar(tile_e[:, 1, :], tile_e[:, 0, :], 1, None, ALU.bitwise_and).then_inc(expert_step, 1)
            dve.wait_ge(expert_step, 2)
            v.tensor_copy(parity[:, 1, :], tile_e[:, 1, :]).then_inc(expert_step, 1)
            v.tensor_scalar(parity[:, 0, :], tile_e[:, 1, :], -1.0, 1.0, ALU.mult, ALU.add).then_inc(expert_step, 1)

            def weights_of_choices():
                dve.wait_ge(lexp_ok, 1)
                v.tensor_reduce(zden[:, 0, :], logit[:, :, :], AX.X, ALU.add).then_inc(w_step, 1)
                for j in range(NJ):
                    i, k = j // K, j % K
                    if j >= 4:
                        dve.wait_ge(pick_ok, j - 3)
                    v.scalar_tensor_tensor(junk[:, j % 4, :], slotmap[:, i, :], slot8[:, i, k:k + 1], logit[:, i, :],
                                           ALU.is_equal, ALU.mult, accum_out=pick[:, j:j + 1]).then_inc(pick_ok, 1)
                dve.wait_ge(pick_ok, NJ)
                pk = pick[:, :].rearrange("p (i k) -> p i k", k=K)
                v.tensor_reduce(zden[:, 1, :], pk, AX.X, ALU.add).then_inc(w_step, 1)
                dve.wait_ge(w_step, 2)
                v.scalar_tensor_tensor(zden[:, 2, :], zden[:, 0, :], 1e-8, zden[:, 1, :], ALU.mult, ALU.add).then_inc(w_step, 1)
                dve.wait_ge(w_step, 3)
                v.reciprocal(zden[:, 0, :], zden[:, 2, :]).then_inc(w_step, 1)
                dve.wait_ge(w_step, 4)
                v.tensor_tensor(wgt[:, :].rearrange("p (i k) -> p i k", k=K), pk,
                                zden[:, 0, :].unsqueeze(2).broadcast_to([P, NT, K]), ALU.mult).then_inc(w_step, 1)

            def unit(n):
                i, hc, blk = unit_of(n)
                dve.wait_ge(unit_sb, 2 * n + 2 if n < 4 else 8 + n - 3)
                u = sgu_v[:, 1, n % 2, :] if n < 4 else pb[2 * (n % 2) + 1][:, :]
                v.tensor_tensor(hsh[:, 2 * i + hc, blk * 512:(blk + 1) * 512], sgu_v[:, 0, n % 2, :], u,
                                ALU.mult).then_inc(unit_v, 1)

            unit(2)
            unit(3)
            dve.wait_ge(expert_step, 4)

            def stages(first, k, have):
                if have(2):
                    q, n = first + (k - 2), (k - 2) % 2
                    dve.wait_ge(silu_ok, q + 1)
                    if have(4):
                        dve.wait_ge(hT_ps, q - 1)
                    for par in range(2):
                        ins = v.scalar_tensor_tensor(hh[:, n, par, :], sg[:, n, :], parity[:, par, bass.ds(q, 1)],
                                                     pb[2 + n][:, F:2 * F], ALU.mult, ALU.mult)
                    ins.then_inc(h_ok, 1)
                if have(0):
                    q, n = first + k, k % 2
                    dve.wait_ge(xT_ps, q + 1)
                    if have(2):
                        dve.wait_ge(gu_ps, q - 1)
                    v.tensor_copy(xgT[:, n, :, :], pb[n][:, 0:D].rearrange("p (c n) -> p c n", c=DC)).then_inc(xT_sb, 1)
                    v.tensor_copy(tok_now[:, k:k + 1], tok[:, bass.ds(next_tile(q), 1)]).then_inc(tok_set, 1)

            def next_tile(q):
                return q + U

            over_tiles(dve, stages, 3)
            weights_of_choices()
            unit(4)
            unit(5)
            dve.wait_ge(w_step, 5)
            for i in range(NT):
                n = i * (K + 1)
                for k in range(K):
                    j = i * K + k
                    dve.wait_ge(back[j % NC], 16 * (j // NC + 1))
                    if k:
                        dve.wait_ge(mixed, n + k)
                    v.scalar_tensor_tensor(xs[:, i, :], z[:, j % NC, :], wgt[:, j:j + 1], xs[:, i, :],
                                           ALU.mult, ALU.add).then_inc(mixed, 1)
                dve.wait_ge(down_ps, i + 1)
                dve.wait_ge(mixed, n + K)
                v.tensor_tensor(xs[:, i, :], pb[4 + i % 2][:, 0:D], xs[:, i, :], ALU.add).then_inc(mixed, 1)
                if i == NT // 2 - 1:
                    unit(6)
                    unit(7)

        @block.tensor
        def _(pe):
            t = nc.tensor
            pe.wait_ge(ld_proj, 16)
            for blk in range(2):
                t.matmul(pb[blk][:, :], proj_sb[0:H, N:N + 2 * H], proj_sb[0:H, blk * 512:(blk + 1) * 512],
                         start=True, stop=True).then_inc(proj_ps, 1)
            for b in range(B):
                pe.wait_ge(qk_sb, 2 * (b // 2 + 1))
                for c in range(TPB):
                    q0 = b * S + c * P
                    ins = t.matmul(pb[4 + b][:, c * S:(c + 1) * S], qkT[0:H, 0, q0:q0 + P], qkT[0:H, 1, b * S:(b + 1) * S],
                                   start=True, stop=True)
                ins.then_inc(score_ps, 1)
            pe.wait_ge(const_ok, 9)

            def logits(b):
                pe.wait_ge(zT_sb, DC * (b + 1))
                if b == 0:
                    pe.wait_ge(ld_router, 16)
                    pe.wait_ge(score_x, 1)
                for c in range(TPB):
                    i = TPB * b + c
                    for h in range(DC):
                        t.matmul(pb[4][:, i * E:(i + 1) * E], zT[:, h, i * P:(i + 1) * P], wr_sb[:, h, :],
                                 start=(i == 0 and h == 0), stop=False, skip_group_check=True)

            def unit(n, g, halves=(0, 1)):
                i, hc, blk = unit_of(n)
                if n == 0 and g == 0:
                    pe.wait_ge(ld_shared, 16)
                if 2 <= n < 6:
                    pe.wait_ge(unit_sb, 2 * (n - 1))
                elif n >= 6:
                    pe.wait_ge(unit_v, n - 3)
                for h in halves:
                    ins = t.matmul(pb[2 * (n % 2) + g][:, :], sgu_sb[:, i, g, h, hc * P:(hc + 1) * P],
                                   zT[:, h, blk * 512:(blk + 1) * 512], start=(h == 0), stop=(h == DC - 1),
                                   skip_group_check=True)
                if g and 1 in halves:
                    ins.then_inc(unit_ps, 1)

            for b in range(B):
                pe.wait_ge(z_ok, TPB * (b + 1))
                for h in range(DC):
                    for c in range(TPB):
                        i = TPB * b + c
                        ins = t.transpose(pb[b][:, h * S + c * P:h * S + (c + 1) * P], z[:, i, h::DC], ident[:, :])
                ins.then_inc(zT_ps, 1)
                if b >= 1:
                    logits(b - 1)
            pe.wait_ge(zT_sb, DC * B)
            pe.wait_ge(score_x, B)
            for h in range(DC):
                ins = t.matmul(pb[5][:, 0:B], te1_sb[:, h, :], zsum[:, h, :], start=(h == 0), stop=(h == DC - 1))
            ins.then_inc(h1_ps, 1)
            logits(B - 1)
            pe.wait_ge(h1_ok, 1)
            t.matmul(pb[5][0:B, 16:16 + ND], h1[:, :], te2_sb, start=True, stop=True).then_inc(tl_ps, 1)
            unit(0, 0)
            pe.wait_ge(task_dve, 5)
            t.transpose(pb[5][0:ND, 32:32 + B], tl[:, 2, :], ident[0:B, 0:B]).then_inc(td_ps, 1)
            pe.wait_ge(tdT_ok, 1)
            pe.wait_ge(ld_task, 16)
            for b in range(B):
                ins = t.matmul(pb[4][:, TPB * b * E:TPB * (b + 1) * E].rearrange("p (i e) -> p i e", e=E), tdT[:, b:b + 1].broadcast_to([ND, P]),
                               aff_sb[:, :].unsqueeze(1).broadcast_to([ND, TPB, E]),
                               start=False, stop=(b == B - 1), skip_group_check=True)
            ins.then_inc(logit_ps, 1)
            unit(0, 1)
            unit(1, 0)
            pe.wait_ge(chosen_ok, 1)
            for i in range(NT):
                ins = t.matmul(pb[6][0:E, 0:P], chosen[:, i, :], ones_bf[:, :], start=(i == 0), stop=(i == NT - 1))
            ins.then_inc(count_ps, 1)
            t.matmul(pb[7][:, :], tri[:, :], chosen[:, :, :].rearrange("p i e -> p (i e)"), start=True, stop=False, skip_group_check=True)
            for i in range(NT - 1):
                t.matmul(pb[7][:, (i + 1) * E:].rearrange("p (i e) -> p i e", e=E), ones_bf[:, :],
                         chosen[:, i, :].unsqueeze(1).broadcast_to([P, NT - 1 - i, E]),
                         start=False, stop=False, skip_group_check=True)
            pe.wait_ge(need_ok, 2)
            t.matmul(pb[7][:, :].rearrange("p (i e) -> p i e", e=E), need_bf[:, :],
                     tri_less[:, :].unsqueeze(1).broadcast_to([E, NT, E]),
                     start=False, stop=True, skip_group_check=True).then_inc(rank_ps, 1)
            t.matmul(pb[5][0:E, 128:129], tri[0:E, 0:E], need_bf[:, 0:1], start=True, stop=True)
            t.matmul(pb[5][0:1, 160:161], need_bf[:, 0:1], ones_bf[0:E, 0:1], start=True, stop=True).then_inc(rank_ps, 1)
            unit(1, 1)
            for r in range(NJ // GJ):
                pe.wait_ge(onehot, 2 * (r + 1))
                pe.wait_ge(valued, 2 * (r + 1))
                for j in range(GJ):
                    ins = t.matmul(pb[6][:, 128:128 + MAXT], oh_lane[:, r % 2, :, j], oh_val[:, r % 2, :, j],
                                   start=(r == 0 and j == 0), stop=(r == NJ // GJ - 1 and j == GJ - 1))
                ins.then_inc(listed, 1)
                if r < 3:
                    unit(2, r // 2, (r % 2,))
            pe.wait_ge(cmp_ok, 2)
            t.matmul(pb[5][:, 192:192 + MAXT], ones_bf[0:E, :], cmp[:, :], start=True, stop=True).then_inc(expert_ps, 1)
            unit(2, 1, (1,))
            unit(3, 0)
            unit(3, 1)
            pe.wait_ge(unit_sb, 2 * 4)

            for n in range(8):
                pe.wait_ge(ld_gu[n], 16)
            for n in range(4):
                pe.wait_ge(ld_d[n], 16)

            def stages(first, k, have):
                if have(0):
                    q = first + k
                    pe.wait_ge(got[k], (first + U) * (16 // U))
                    if have(2):
                        pe.wait_ge(xT_sb, q - 1)
                    for h in range(DC):
                        ins = t.transpose(pb[k % 2][:, h * P:(h + 1) * P], xg[:, k, h::DC], ident[:, :])
                    ins.then_inc(xT_ps, 1)
                if k % 4 == 0:
                    gu_of[k:k + 4] = load_at(gu_at, first + k)
                if have(1):
                    q, n = first + (k - 1), (k - 1) % 2
                    pe.wait_ge(xT_sb, q + 1)
                    if have(3):
                        pe.wait_ge(h_ok, q - 1)
                    for h in range(DC):
                        ins = t.matmul(pb[2 + n][:, 0:2 * F], xgT[:, n, h, :],
                                       wgu_sb[:, bass.ds(gu_of[k], 1), h, :].rearrange("p o f -> p (o f)"),
                                       start=(h == 0), stop=(h == DC - 1))
                    ins.then_inc(gu_ps, 1)
                if k == 0:
                    d_of[0:D_LAG] = load_at(d_at, first)
                elif k >= D_LAG:
                    d_of[k] = gu_of[k - D_LAG + GU_LAG] // 2
                if have(3):
                    q, n = first + (k - 3), (k - 3) % 2
                    pe.wait_ge(h_ok, q + 1)
                    if have(4):
                        pe.wait_ge(hT_sb, q)
                    t.transpose(pb[6][:, 0:P], hh[:, n, :, :].rearrange("p a f -> p (a f)"), ident[:, :]).then_inc(hT_ps, 1)
                if have(4):
                    q, n = first + (k - 4), (k - 4) % 2
                    pe.wait_ge(hT_sb, q + 1)
                    if have(6):
                        pe.wait_ge(y_sb, q - 1)
                    t.matmul(pb[4 + n][:, 0:D], hT[:, n, :],
                             wd_sb[:, bass.ds(d_of[k], 1), :].rearrange("p o d -> p (o d)"),
                             start=True, stop=True).then_inc(y_ps, 1)

            gu_of, d_of = [None] * U, [None] * U

            def load_at(table, first):
                _, vals = nc.values_load_multi_w_load_instructions(
                    table[0:1, bass.ds(first, 4)], engines=[mybir.EngineType.PE], min_val=0,
                    max_val=(E if table is gu_at else E // 2) - 1,
                    skip_runtime_bounds_check_because="VectorE has bounded the expert of every tile by E - 1")
                return vals

            pe.wait_ge(at_ok, 4)
            end = over_tiles(pe, stages, 5)
            pe.wait_ge(xT_sb, end)
            pe.wait_ge(h_ok, end)
            pe.wait_ge(y_sb, end)

            def shared_out(i):
                if i >= 2:
                    pe.wait_ge(mixed, (i - 1) * (K + 1))
                for q in range(NSH * DC):
                    ins = t.matmul(pb[4 + i % 2][:, 0:D], hsh[:, q, i * P:(i + 1) * P], sd_sb[:, q, :],
                                   start=(q == 0), stop=(q == NSH * DC - 1))
                ins.then_inc(down_ps, 1)

            pe.wait_ge(unit_h, 2)
            for blk in range(2):
                for n in (4 + 2 * blk, 5 + 2 * blk):
                    unit(n, 0)
                    unit(n, 1)
                pe.wait_ge(unit_v, 4 + 2 * blk)
                for i in range(blk * NT // 2, (blk + 1) * NT // 2):
                    shared_out(i)


def kernel(x, ctx_512, mask_SxS2_bk1, mask_BxS2_bf0, L0_xattn_Wq, L0_xattn_bq, L0_xattn_Wk, L0_xattn_bk,
           L0_ffn_Wr, L0_ffn_router_bias, L0_ffn_affinity, L0_ffn_te_W1, L0_ffn_te_b1, L0_ffn_te_W2,
           L0_ffn_te_b2, L0_ffn_Wg, L0_ffn_Wu, L0_ffn_Wd, L0_ffn_Sg, L0_ffn_Su, L0_ffn_Sd):
    import numpy as np
    import concourse.bacc as bacc
    from concourse.bass_utils import run_bass_kernel_spmd

    def by_feature(w):
        return w.reshape(P, DC, -1)

    sgu = np.stack([np.stack([by_feature(L0_ffn_Sg[i]), by_feature(L0_ffn_Su[i])], 1) for i in range(NSH)], 1)
    sd = L0_ffn_Sd.reshape(NSH * DC, P, D).transpose(1, 0, 2)
    arrays = {
        "x": x.reshape(N, D),
        "proj": np.concatenate([ctx_512.reshape(N, H).T, L0_xattn_Wq.T, L0_xattn_Wk.T,
                                L0_xattn_bq[:, None], L0_xattn_bk[:, None]], 1),
        "amask": mask_SxS2_bk1,
        "kmask": mask_BxS2_bf0.reshape(B * S),
        "router": np.concatenate([by_feature(L0_ffn_Wr.T).reshape(P, -1), by_feature(L0_ffn_te_W1.T).reshape(P, -1),
                                  L0_ffn_te_W2.T, L0_ffn_te_b1[:, None]], 1),
        "task": L0_ffn_affinity.T,
        "b2": L0_ffn_te_b2,
        "rbias": L0_ffn_router_bias,
        "shared": np.concatenate([sgu.reshape(P, -1), sd.reshape(P, -1)], 1),
        "wgu": np.stack([L0_ffn_Wg.reshape(E, P, DC, F), L0_ffn_Wu.reshape(E, P, DC, F)], 3).reshape(E, P, -1),
        "wd": L0_ffn_Wd,
    }
    arrays = {k: np.ascontiguousarray(v) for k, v in arrays.items()}
    nc = bacc.Bacc("TRN2", target_bir_lowering=False, num_devices=1)
    aps = {k: nc.dram_tensor(f"in_{k}", v.shape, mybir.dt.from_np(v.dtype), kind="ExternalInput").ap() for k, v in arrays.items()}
    out = nc.dram_tensor("out", (N, D), F32, kind="ExternalOutput").ap()
    build_xattn_moe(nc, *aps.values(), out)
    r = run_bass_kernel_spmd(nc, [{f"in_{k}": v for k, v in arrays.items()}], core_ids=[0])
    return r.results[0]["out"].reshape(B, S, D)
```

```python
from contextlib import ExitStack

import concourse.bass as bass
from concourse import mybir

F32 = mybir.dt.float32
F16 = mybir.dt.float16
BF16 = mybir.dt.bfloat16
I32 = mybir.dt.int32
U32 = mybir.dt.uint32
U8 = mybir.dt.uint8
ALU = mybir.AluOpType
ACT = mybir.ActivationFunctionType
AX = mybir.AxisListType

P = 128
B, S, D = 4, 256, 256
H = 64
E, F, K, ND = 64, 64, 4, 4
NSH, HSH = 2, 256
N = B * S
NT = N // P
TPB = S // P
DC = D // P
MAXT = 96
SLOTS = MAXT * P
NJ = NT * K
GJ = 2 * K
BIG = 1e30
SENTINEL = -3e38
CHOSEN = 3e38
ROUND = 12582912.0
SKIP = 5001.0
EPS = 1e-5

U = 12
XB = 6
FILL_TURNS = 2
FILL_TILE = N * K // P + FILL_TURNS * U * 3 // 2
YB = 4
GU_LAG, D_LAG = 1, 4
LG_BANK = (4, 6)
NC = 8
EARLY = 2


def build_xattn_moe(nc, x, proj, amask, kmask, router, task, b2, rbias, shared, wgu, wd, out):
    z_dram = nc.dram_tensor("z_rows", (N, D), F32, kind="Internal").ap()
    y_dram = nc.dram_tensor("y_slots", (SLOTS, D), F32, kind="Internal").ap()

    with ExitStack() as ctx:
        def sb(name, shape, dt=F32):
            return ctx.enter_context(nc.sbuf_tensor(name, shape, dt))

        def sem(name):
            return ctx.enter_context(nc.semaphore(name))

        wgu_sb = sb("wgu_sb", [P, E, DC, 2 * F])
        wd_sb = sb("wd_sb", [P, E // 2, D])
        shared_sb = sb("shared_sb", [P, NSH * 2 * DC * HSH + NSH * DC * D])
        sgu_sb = shared_sb[:, 0:NSH * 2 * DC * HSH].rearrange("p (i g c h) -> p i g c h", i=NSH, g=2, c=DC)
        sd_sb = shared_sb[:, NSH * 2 * DC * HSH:].rearrange("p (q d) -> p q d", d=D)
        proj_sb = sb("proj_sb", [P, N + 2 * H + 2])
        router_sb = sb("router_sb", [P, DC * E + DC * P + ND + 1])
        wr_sb = router_sb[:, 0:DC * E].rearrange("p (c e) -> p c e", c=DC)
        te1_sb = router_sb[:, DC * E:DC * (E + P)].rearrange("p (c j) -> p c j", c=DC)
        te2_sb = router_sb[:, DC * (E + P):DC * (E + P) + ND]
        b1_sb = router_sb[:, DC * (E + P) + ND:]
        aff_sb = sb("aff_sb", [ND, E])
        b2_sb = sb("b2_sb", [B, ND])
        rb_sb = sb("rb_sb", [P, E])
        amask_sb = sb("amask_sb", [P, TPB, S], U8)
        kmask_sb = sb("kmask_sb", [P, B * S], U8)

        xs = sb("xs", [P, NT, D])
        z = sb("z", [P, NT, D])
        zT = sb("zT", [P, DC, N])
        hsh = sb("hsh", [P, NSH * DC, N])
        qc = hsh[:, 0:2, :].rearrange("p a n -> p (a n)").rearrange("p (i d) -> p i d", d=D)
        mb = hsh[:, 2:4, :].rearrange("p a (b s) -> p a b s", b=B)
        qkT = sb("qkT", [P, 2, N])
        sgu_v = qkT[:, :, :].rearrange("p a (r n) -> p a r n", r=2)
        sc = sb("sc", [P, 2, TPB, S])
        kneg = z[:, 0:B, :].rearrange("p b t -> p (b t)")
        aneg = z[:, B:B + TPB, :]
        xg = sb("xg", [P, XB, D])
        xgT = sb("xgT", [P, 2, DC, P])
        sg = sb("sg", [P, 2, F])
        hh = sb("hh", [P, 2, 2, F])
        hT = sb("hT", [P, 2, P])
        ysb = sb("ysb", [P, YB, D])
        zero_row = sb("zero_row", [P, D])
        tok_now = sb("tok_now", [P, XB], U32)

        ident = sb("ident", [P, P])
        ones_bf = sb("ones_bf", [P, P], BF16)
        tri = sb("tri", [P, P], BF16)
        tri_less = sb("tri_less", [E, E], BF16)
        lanes = sb("lanes", [P, P, GJ], F16)
        tok_no = sb("tok_no", [P, NT])

        st = sb("st", [P, NT, 6])
        mv1 = sb("mv1", [P, NT, 2])
        mv2 = sb("mv2", [P, NT, 2])
        rstd1 = sb("rstd1", [P, NT])
        rstd2 = sb("rstd2", [P, NT])
        nmr1 = sb("nmr1", [P, NT])
        nmr2 = sb("nmr2", [P, NT])
        veps = sb("veps", [P, 2, NT])
        mhalf = sb("mhalf", [P, NT])
        smax = sb("smax", [P, NT])
        nmax = sb("nmax", [P, NT])
        ssum = sb("ssum", [P, NT])
        skeep = sb("skeep", [P, NT])
        rinv = sb("rinv", [P, NT])
        zsum = sb("zsum", [P, DC, B])
        h1 = sb("h1", [P, B])
        warm = sb("warm", [1, 2])
        tl = sb("tl", [B, 4, ND])
        ts_ = sb("ts_", [B, 4])
        tdT = sb("tdT", [ND, B])
        lb = proj_sb[:, 0:NT * (E + 4)].rearrange("p (i e) -> p i e", i=NT)
        marked = proj_sb[:, NT * (E + 4):2 * NT * (E + 4)].rearrange("p (i e) -> p i e", i=NT)
        top8 = sb("top8", [P, NT, 8])
        chosen = sb("chosen", [P, NT, E], BF16)
        logit = sb("logit", [P, NT, E])
        lmax = sb("lmax", [P, NT])
        slotmap = sb("slotmap", [P, NT, E])
        need = sb("need", [E, 2, P])
        need_bf = sb("need_bf", [E, P], BF16)
        slot8 = sb("slot8", [P, NT, 8])
        slot_i = sb("slot_i", [P, 3, NJ], I32)
        slot_h = sb("slot_h", [P, 2, NJ], F16)
        oh_lane = (sc[:, :, :, :].rearrange("p a c s -> p (a c s)").bitcast(F16)
                   .rearrange("p (n l j) -> p n l j", n=2, j=GJ))
        oh_tile = sb("oh_tile", [P, 2, MAXT, GJ], F16)
        oh_val = sb("oh_val", [P, 2, MAXT, GJ], F16)
        empty = sb("empty", [P, MAXT])
        tok = sb("tok", [P, MAXT + XB], U32)
        cuml = sb("cuml", [E, 1])
        cmp = sb("cmp", [E, MAXT], BF16)
        tile_e = sb("tile_e", [P, 2, MAXT], I32)
        gu_at = sb("gu_at", [1, MAXT + U], I32)
        parity = sb("parity", [P, 2, MAXT])
        turns_f = sb("turns_f", [1, 1])
        turns = sb("turns", [1, 2], I32)
        pick = sb("pick", [P, NJ])
        junk = sc[:, 1, :, :].rearrange("p c s -> p (c s)").rearrange("p (n e) -> p n e", e=E)
        zden = sb("zden", [P, 3, NT])
        wgt = sb("wgt", [P, NJ])

        pb = [ctx.enter_context(nc.psum_tensor(f"pb{i}", [P, 512], F32)) for i in range(8)]

        ld_proj, ld_mask, ld_router = sem("ld_proj"), sem("ld_mask"), sem("ld_router")
        ld_task, ld_b2, ld_rb, ld_shared, ld_kmask = sem("ld_task"), sem("ld_b2"), sem("ld_rb"), sem("ld_shared"), sem("ld_kmask")
        ld_x = [sem(f"ld_x{b}") for b in range(B)]
        ld_gu = [sem(f"ld_gu{n}") for n in range(8)]
        ld_d = [sem(f"ld_d{n}") for n in range(4)]
        const_ok, warm_ok, aneg_ok, mask_ok = sem("const_ok"), sem("warm_ok"), sem("aneg_ok"), sem("mask_ok")
        proj_ps, qk_sb = sem("proj_ps"), sem("qk_sb")
        stat1, mv1_ok, var1, rstd1_ok, nmr1_ok, qc_ok = sem("stat1"), sem("mv1_ok"), sem("var1"), sem("rstd1_ok"), sem("nmr1_ok"), sem("qc_ok")
        score_ps, score_x, score_m, nmax_ok, exp_ok = (sem("score_ps"), sem("score_x"), sem("score_m"), sem("nmax_ok"), sem("exp_ok"))
        keep_ok, rinv_ok, x1_ok = sem("keep_ok"), sem("rinv_ok"), sem("x1_ok")
        stat2, mv2_ok, var2, rstd2_ok, nmr2_ok, z_ok = (
            sem("stat2"), sem("mv2_ok"), sem("var2"), sem("rstd2_ok"), sem("nmr2_ok"), sem("z_ok"))
        z_out = sem("z_out")
        zT_ps, zT_sb = sem("zT_ps"), sem("zT_sb")
        h1_ps, h1_ok, tl_ps, task_dve, task_exp, td_ps, tdT_ok = (
            sem("h1_ps"), sem("h1_ok"), sem("tl_ps"), sem("task_dve"), sem("task_exp"), sem("td_ps"), sem("tdT_ok"))
        logit_ps, lb_ok, top_ok, cut_ok, marked_ok, chosen_ok = (
            sem("logit_ps"), sem("lb_ok"), sem("top_ok"), sem("cut_ok"), sem("marked_ok"), sem("chosen_ok"))
        count_ps, need_ok, rank_ps, slot_ok = sem("count_ps"), sem("need_ok"), sem("rank_ps"), sem("slot_ok")
        slot8_ok, slotf, onehot, valued, listed, tok_step = (
            sem("slot8_ok"), sem("slotf"), sem("onehot"), sem("valued"), sem("listed"), sem("tok_step"))
        cmp_ok, turns_step, expert_ps, expert_step, at_ok = sem("cmp_ok"), sem("turns_step"), sem("expert_ps"), sem("expert_step"), sem("at_ok")
        logit_sb, lmax_ok, lsub_ok, lexp_ok = sem("logit_sb"), sem("lmax_ok"), sem("lsub_ok"), sem("lexp_ok")
        unit_ps, unit_sb, unit_h = sem("unit_ps"), sem("unit_sb"), sem("unit_h")
        got = [sem(f"got{n}") for n in range(XB)]
        xT_ps, xT_sb, tok_set, gu_ps, silu_ok, h_ok, hT_ps, hT_sb, y_ps, y_sb = (
            sem("xT_ps"), sem("xT_sb"), sem("tok_set"), sem("gu_ps"), sem("silu_ok"), sem("h_ok"), sem("hT_ps"),
            sem("hT_sb"), sem("y_ps"), sem("y_sb"))
        zeroed, y_fill = sem("zeroed"), sem("y_fill")
        y_out = [sem(f"y_out{n}") for n in range(YB)]
        back = [sem(f"back{n}") for n in range(NC)]
        pick_ok, w_step = sem("pick_ok"), sem("w_step")
        down_ps, mixed, shared_in, out_ok = sem("down_ps"), sem("mixed"), sem("shared_in"), sem("out_ok")

        def x_rows(dram, b):
            return dram[b * S:(b + 1) * S, :].rearrange("(c p) d -> p c d", p=P)

        def turn_count(eng):
            eng.wait_ge(turns_step, 3)
            return eng.value_load(turns[0:1, 0:1], min_val=-(-N * K // P // U), max_val=MAXT // U)

        def last_turn_end(eng):
            return eng.value_load(turns[0:1, 1:2], min_val=-(-N * K // P // U) * U - 2 * U, max_val=MAXT - 2 * U) + 2 * U

        units = [(0, 0, 0), (0, 0, 1), (0, 1, 0), (1, 0, 0), (1, 1, 0), (0, 1, 1), (1, 0, 1), (1, 1, 1)]

        block = ctx.enter_context(nc.Block())

        def over_tiles(eng, stages, lags, counts=None):
            if counts is None:
                counts = turn_count(eng), last_turn_end(eng)
            n_turns, end = counts
            for k in range(U):
                stages(0, 0, k, lambda lag: k >= lag)
            with eng.Fori(1, n_turns) as turn:
                for k in range(U):
                    stages(turn, turn * U, k, lambda lag: True)
            for k in range(lags - 1):
                stages(n_turns, end, k, lambda lag: k < lag)
            return end

        @block.sync
        def _(sp):
            sp.dma_start(proj_sb[0:H, :], proj).then_inc(ld_proj, 16)
            sp.dma_start(xs[:, 0:TPB, :], x_rows(x, 0)).then_inc(ld_x[0], 16)
            sp.dma_start(kmask_sb[:, :], kmask.partition_broadcast(P)).then_inc(ld_kmask, 16)
            sp.dma_start(amask_sb[:, :, :], amask.rearrange("(c p) t -> p c t", p=P)).then_inc(ld_mask, 16)
            for b in range(1, B):
                sp.dma_start(xs[:, TPB * b:TPB * (b + 1), :], x_rows(x, b)).then_inc(ld_x[b], 16)
            sp.dma_start(router_sb[:, :], router).then_inc(ld_router, 16)
            sp.dma_start(aff_sb[:, :], task).then_inc(ld_task, 16)
            sp.dma_start(b2_sb[:, :], b2.partition_broadcast(B)).then_inc(ld_b2, 16)
            sp.dma_start(rb_sb[:, :], rbias.partition_broadcast(P)).then_inc(ld_rb, 16)
            sp.dma_start(shared_sb[:, :], shared).then_inc(ld_shared, 16)

            def load_weights(n):
                sp.dma_start(wgu_sb[:, 8 * n:8 * (n + 1), :, :].rearrange("p e c f -> p e (c f)"),
                             wgu[8 * n:8 * (n + 1), :, :].rearrange("e p n -> p e n")).then_inc(ld_gu[n], 16)
                if n % 2 == 0:
                    q = 4 * n
                    sp.dma_start(wd_sb[:, q:q + 8, :],
                                 wd[2 * q:2 * q + 16, :, :].rearrange("(q a) f d -> (a f) q d", a=2)).then_inc(ld_d[n // 2], 16)
            for n in range(4):
                load_weights(n)
            for b in range(B):
                sp.wait_ge(z_ok, TPB * (b + 1))
                sp.dma_start(x_rows(z_dram, b), z[:, TPB * b:TPB * (b + 1), :]).then_inc(z_out, 16)
                load_weights(4 + b)
            sp.wait_ge(zeroed, 2)
            with sp.Fori(FILL_TILE, MAXT) as tile:
                sp.dma_start(y_dram[bass.ds(tile * P, P), :], zero_row[:, :]).then_inc(y_fill, 16)
            n_turns = turn_count(sp)

            def store(first, k):
                sp.wait_ge(y_sb, first + k + 1)
                sp.dma_start(y_dram[bass.ds((first + k) * P, P), :], ysb[:, k % YB, :]).then_inc(y_out[k % YB], 16)

            def store_and_fill(turn, k):
                store(turn * U, k)
                n = 1 + k % 2
                tile = turn * (U // 2 * 3) + (k // 2 * 3 + k % 2 + N * K // P)
                sp.dma_start(y_dram[bass.ds(tile * P, n * P), :].rearrange("(u p) d -> p u d", p=P),
                             zero_row[:, :].unsqueeze(1).broadcast_to([P, n, D])).then_inc(y_fill, 16)

            for k in range(U):
                store_and_fill(0, k)
            with sp.Fori(1, FILL_TURNS) as turn:
                for k in range(U):
                    store_and_fill(turn, k)
            with sp.Fori(FILL_TURNS, n_turns) as turn:
                for k in range(U):
                    if k == N * K // P - FILL_TURNS * U:
                        sp.wait_ge(y_fill, 16 * (MAXT - FILL_TILE + FILL_TURNS * U))
                    store(turn * U, k)
            for i in range(NT):
                sp.wait_ge(mixed, (i + 1) * K)
                sp.wait_ge(shared_in, i + 1)
                sp.dma_start(out[i * P:(i + 1) * P, :], xs[:, i, :]).then_inc(out_ok, 16)
            sp.wait_ge(out_ok, 16 * NT)

        @block.gpsimd
        def _(pool):
            g = nc.gpsimd
            g.memset(mhalf[:, :], -0.5).then_inc(const_ok, 1)
            g.memset(warm[:, :], 0.0).then_inc(warm_ok, 1)
            g.memset(ident[:, :], 0.0).then_inc(const_ok, 1)
            g.memset(ones_bf[:, :], 1.0).then_inc(const_ok, 1)
            g.iota(lanes[:, :, :], [[1, P], [0, GJ]], base=0, channel_multiplier=0, allow_small_or_imprecise_dtypes=True).then_inc(const_ok, 1)
            g.iota(tok_no[:, :], [[P, NT]], base=1, channel_multiplier=1, allow_small_or_imprecise_dtypes=True).then_inc(const_ok, 1)
            pool.wait_ge(const_ok, 3)
            g.affine_select(out=ident[:, :], in_=ident[:, :], compare_op=ALU.not_equal, fill=1.0, base=0,
                            pattern=[[-1, P]], channel_multiplier=1).then_inc(const_ok, 1)
            g.affine_select(out=tri[:, :], in_=ones_bf[:, :], compare_op=ALU.is_ge, fill=0.0, base=0,
                            pattern=[[1, P]], channel_multiplier=-1).then_inc(const_ok, 1)
            g.memset(tri_less[:, :], float(P)).then_inc(const_ok, 1)
            pool.wait_ge(const_ok, 8)
            g.affine_select(out=tri_less[:, :], in_=tri_less[:, :], compare_op=ALU.is_gt, fill=0.0, base=0,
                            pattern=[[1, E]], channel_multiplier=-1).then_inc(const_ok, 1)

            def add_masks(b):
                if b == 0:
                    pool.wait_ge(aneg_ok, 1)
                    pool.wait_ge(mask_ok, 1)
                g.tensor_tensor(mb[:, :, b, :], aneg, kneg[:, b * S:(b + 1) * S].unsqueeze(1).broadcast_to([P, TPB, S]),
                                ALU.add).then_inc(mask_ok, 1)

            for b in range(B):
                t = slice(TPB * b, TPB * (b + 1))
                pool.wait_ge(var1, b + 1)
                g.tensor_tensor(rstd1[:, t], veps[:, 0, t], mhalf[:, t], ALU.pow).then_inc(rstd1_ok, 1)
                if b >= 1:
                    add_masks(b - 1)
            add_masks(B - 1)
            for b in range(B):
                pool.wait_ge(var2, b + 1)
                t = slice(TPB * b, TPB * (b + 1))
                g.tensor_tensor(rstd2[:, t], veps[:, 1, t], mhalf[:, t], ALU.pow).then_inc(rstd2_ok, 1)

            pool.wait_ge(lmax_ok, 1)
            g.tensor_tensor(logit[:, :, :], logit[:, :, :], lmax[:, :].unsqueeze(2).broadcast_to([P, NT, E]),
                            ALU.subtract).then_inc(lsub_ok, 1)

            pool.wait_ge(z_out, 16 * B)
            pool.wait_ge(zeroed, 1)

            tile_no = ctx.enter_context(pool.register("tile_no"))
            pool.reg_mov(tile_no, 1)

            def gather(k):
                pool.wait_ge(tok_set, tile_no)
                pool.reg_add(tile_no, tile_no, 1)
                n = k % XB
                g.indirect_dma_start(xg[:, n, :], None, z_dram, bass.IndirectOffsetOnAxis(ap=tok_now[:, n:n + 1], axis=0),
                                     bounds_check=N - 1, oob_is_err=False).then_inc(got[n], 16)

            for k in range(U):
                gather(k)
            n_turns = turn_count(pool)
            with pool.Fori(1, n_turns) as _:
                for k in range(U):
                    gather(k)
            for n in range(YB):
                pool.wait_ge(y_out[n], n_turns * (16 * U // YB))
            last_row = n_turns * (U * P) - 1
            for j in range(NJ):
                if j >= NC:
                    pool.wait_ge(mixed, j - NC + 1)
                g.indirect_dma_start(z[:, j % NC, :], None, y_dram,
                                     bass.IndirectOffsetOnAxis(ap=slot_i[:, 0, j:j + 1].bitcast(U32), axis=0),
                                     bounds_check=last_row, oob_is_err=False).then_inc(back[j % NC], 16)

        def evac_zT(act, b):
            act.wait_ge(zT_ps, b + 1)
            for c in range(DC):
                nc.scalar.activation(zT[:, c, b * S:(b + 1) * S], pb[b][:, c * S:(c + 1) * S], ACT.Identity,
                                     accum_out=zsum[:, c, b:b + 1]).then_inc(zT_sb, 1)

        @block.scalar
        def _(act):
            a = nc.scalar
            for blk in range(2):
                if blk == 1:
                    act.wait_ge(ld_mask, 16)
                    a.activation(aneg, amask_sb[:, :, :], ACT.Identity, scale=-BIG).then_inc(aneg_ok, 1)
                act.wait_ge(proj_ps, blk + 1)
                for w in range(2):
                    a.activation(qkT[0:H, w, blk * 512:(blk + 1) * 512], pb[blk][w * H:(w + 1) * H, :], ACT.Identity,
                                 bias=proj_sb[0:H, N + 2 * H + w:N + 2 * H + w + 1]).then_inc(qk_sb, 1)
            for i in range(NT):
                act.wait_ge(nmr1_ok, i // TPB + 1)
                a.activation(qc[:, i, :], xs[:, i, :], ACT.Identity, bias=nmr1[:, i:i + 1], scale=rstd1[:, i:i + 1]).then_inc(qc_ok, 1)

            def normalise(b):
                act.wait_ge(nmr2_ok, b + 1)
                for c in range(TPB):
                    i = TPB * b + c
                    a.activation(z[:, i, :], xs[:, i, :], ACT.Identity, bias=nmr2[:, i:i + 1], scale=rstd2[:, i:i + 1]).then_inc(z_ok, 1)

            for b in range(B):
                for c in range(TPB):
                    i = TPB * b + c
                    act.wait_ge(nmax_ok, b + 1)
                    a.activation(sc[:, b % 2, c, :], sc[:, b % 2, c, :], ACT.Exp, bias=nmax[:, i:i + 1],
                                 accum_out=ssum[:, i:i + 1]).then_inc(exp_ok, 1)
                if b >= 1:
                    normalise(b - 1)
                if b >= 2:
                    evac_zT(act, b - 2)
            act.wait_ge(warm_ok, 1)
            a.activation(warm[:, 1:2], warm[:, 0:1], ACT.Gelu)
            normalise(B - 1)
            evac_zT(act, B - 2)
            evac_zT(act, B - 1)
            act.wait_ge(h1_ps, 1)
            a.activation(h1[:, :], pb[5][:, 0:B], ACT.Gelu, bias=b1_sb, scale=1.0 / S).then_inc(h1_ok, 1)
            act.wait_ge(task_dve, 3)
            a.activation(tl[:, 1, :], tl[:, 0, :], ACT.Exp, bias=ts_[:, 1:2], accum_out=ts_[:, 2:3]).then_inc(task_exp, 1)
            for half in range(2):
                act.wait_ge(lb_ok, 2 + half)
                a.activation(logit[:, 4 * half:4 * half + 4, :],
                             pb[LG_BANK[half]][:, 0:4 * E].rearrange("p (i e) -> p i e", e=E), ACT.Identity).then_inc(logit_sb, 1)
            act.wait_ge(lsub_ok, 1)
            a.activation(logit[:, :, :], logit[:, :, :], ACT.Exp).then_inc(lexp_ok, 1)

            def unit(n):
                act.wait_ge(unit_ps, n + 1)
                if n >= 2:
                    act.wait_ge(unit_h, n - 1)
                bank = 2 * (n % 2)
                a.activation(sgu_v[:, 0, n % 2, :], pb[bank][:, :], ACT.Silu).then_inc(unit_sb, 1)
                if n < EARLY:
                    a.activation(sgu_v[:, 1, n % 2, :], pb[bank + 1][:, :], ACT.Identity).then_inc(unit_sb, 1)

            def value(r):
                n = r % 2
                act.wait_ge(onehot, 2 * r + 1)
                if r >= 2:
                    act.wait_ge(listed, r - 1)
                for c in range(GJ // K):
                    i = r * GJ // K + c
                    a.activation(oh_val[:, n, :, c * K:(c + 1) * K], oh_tile[:, n, :, c * K:(c + 1) * K], ACT.Identity,
                                 scale=tok_no[:, i:i + 1]).then_inc(valued, 1)

            unit(0)
            for r in range(NJ // GJ):
                value(r)
            counts = turn_count(act), last_turn_end(act)
            unit(1)

            def stages(turn, first, k, have):
                if have(5):
                    q, n = first + (k - 5), (k - 5) % YB
                    act.wait_ge(y_ps, q + 1)
                    if have(5 + YB):
                        act.wait_ge(y_out[n], (first + (k - 5 - n)) * (16 // YB))
                    a.activation(ysb[:, n, :], pb[4 + n % 2][:, 0:D], ACT.Identity).then_inc(y_sb, 1)
                if have(1):
                    q, n = first + (k - 1), (k - 1) % 2
                    act.wait_ge(gu_ps, q + 1)
                    if have(3):
                        act.wait_ge(h_ok, q - 1)
                    a.activation(sg[:, n, :], pb[2 + n][:, 0:F], ACT.Silu).then_inc(silu_ok, 1)
                if have(3):
                    q, n = first + (k - 3), (k - 3) % 2
                    act.wait_ge(hT_ps, q + 1)
                    if have(5):
                        act.wait_ge(y_ps, q - 1)
                    a.activation(hT[:, n, :], pb[6][:, 0:P], ACT.Identity).then_inc(hT_sb, 1)

            over_tiles(act, stages, 6, counts)
            for n in range(EARLY, len(units)):
                unit(n)

        @block.vector
        def _(dve):
            v = nc.vector
            v.memset(xg[:, :, :], 0.0).then_inc(zeroed, 1)
            v.memset(zero_row[:, :], 0.0).then_inc(zeroed, 1)
            v.memset(gu_at[:, :], 0).then_inc(at_ok, 1)
            v.memset(tok[:, MAXT:], 0).then_inc(tok_step, 1)

            def stats(b):
                t = slice(TPB * b, TPB * (b + 1))
                dve.wait_ge(ld_x[b], 16)
                for i in range(TPB * b, TPB * (b + 1)):
                    v.bn_stats(st[:, i, :], xs[:, i, :]).then_inc(stat1, 1)
                for i in range(TPB * b, TPB * (b + 1)):
                    dve.wait_ge(stat1, i + 1)
                    v.bn_aggr(mv1[:, i, :], st[:, i, :]).then_inc(mv1_ok, 1)
                dve.wait_ge(mv1_ok, TPB * (b + 1))
                v.tensor_scalar(veps[:, 0, t], mv1[:, t, 1], EPS, None, ALU.add).then_inc(var1, 1)

            def shift1(b):
                t = slice(TPB * b, TPB * (b + 1))
                dve.wait_ge(rstd1_ok, b + 1)
                v.scalar_tensor_tensor(nmr1[:, t], mv1[:, t, 0], -1.0, rstd1[:, t], ALU.mult, ALU.mult).then_inc(nmr1_ok, 1)

            def scores(b):
                sl = sc[:, b % 2, :, :]
                dve.wait_ge(score_ps, b + 1)
                dve.wait_ge(qc_ok, TPB * (b + 1))
                if b >= 2:
                    dve.wait_ge(x1_ok, TPB * (b - 1))
                v.scalar_tensor_tensor(sl, pb[4 + b][:, :].rearrange("p (c t) -> p c t", c=TPB), float(H) ** -0.5,
                                       qc[:, TPB * b:TPB * (b + 1), :], ALU.mult, ALU.mult).then_inc(score_x, 1)
                dve.wait_ge(score_x, b + 1)
                dve.wait_ge(mask_ok, 2 + b)
                for c in range(TPB):
                    i = TPB * b + c
                    v.tensor_tensor_reduce(sc[:, b % 2, c, :], sc[:, b % 2, c, :], mb[:, c, b, :], 1.0, SENTINEL,
                                           ALU.add, ALU.max, smax[:, i:i + 1]).then_inc(score_m, 1)
                t = slice(TPB * b, TPB * (b + 1))
                dve.wait_ge(score_m, TPB * (b + 1))
                v.tensor_scalar(nmax[:, t], smax[:, t], -1.0, None, ALU.mult).then_inc(nmax_ok, 1)

            def finish(b):
                t = slice(TPB * b, TPB * (b + 1))
                dve.wait_ge(exp_ok, TPB * (b + 1))
                v.scalar_tensor_tensor(skeep[:, t], smax[:, t], -0.5 * BIG, ssum[:, t], ALU.is_gt, ALU.mult).then_inc(keep_ok, 1)
                dve.wait_ge(keep_ok, b + 1)
                v.reciprocal(rinv[:, t], skeep[:, t]).then_inc(rinv_ok, 1)
                dve.wait_ge(rinv_ok, b + 1)
                for c in range(TPB):
                    i = TPB * b + c
                    v.scalar_tensor_tensor(xs[:, i, :], sc[:, b % 2, c, :], rinv[:, i:i + 1], xs[:, i, :],
                                           ALU.mult, ALU.add).then_inc(x1_ok, 1)
                for c in range(TPB):
                    i = TPB * b + c
                    dve.wait_ge(x1_ok, i + 1)
                    v.bn_stats(st[:, i, :], xs[:, i, :]).then_inc(stat2, 1)
                for c in range(TPB):
                    i = TPB * b + c
                    dve.wait_ge(stat2, i + 1)
                    v.bn_aggr(mv2[:, i, :], st[:, i, :]).then_inc(mv2_ok, 1)
                dve.wait_ge(mv2_ok, TPB * (b + 1))
                v.tensor_scalar(veps[:, 1, t], mv2[:, t, 1], EPS, None, ALU.add).then_inc(var2, 1)

            def shift2(b):
                t = slice(TPB * b, TPB * (b + 1))
                dve.wait_ge(rstd2_ok, b + 1)
                v.scalar_tensor_tensor(nmr2[:, t], mv2[:, t, 0], -1.0, rstd2[:, t], ALU.mult, ALU.mult).then_inc(nmr2_ok, 1)

            stats(0)
            dve.wait_ge(ld_kmask, 16)
            v.tensor_scalar(kneg[:, :], kmask_sb[:, :], -BIG, None, ALU.mult).then_inc(mask_ok, 1)
            stats(1)
            shift1(0)
            stats(2)
            shift1(1)
            stats(3)
            scores(0)
            shift1(2)
            scores(1)
            shift1(3)
            finish(0)
            for b in range(2, B):
                scores(b)
                if b == 2:
                    dve.wait_ge(mask_ok, 1 + B)
                shift2(b - 2)
                finish(b - 1)
            shift2(B - 2)
            finish(B - 1)
            shift2(B - 1)

            v.memset(lb[:, :, E:E + 4], SENTINEL).then_inc(lb_ok, 1)
            dve.wait_ge(tl_ps, 1)
            dve.wait_ge(ld_b2, 16)
            v.tensor_tensor(tl[:, 0, :], pb[5][0:B, 16:16 + ND], b2_sb[:, :], ALU.add).then_inc(task_dve, 1)
            dve.wait_ge(task_dve, 1)
            v.tensor_reduce(ts_[:, 0:1], tl[:, 0, :], AX.X, ALU.max).then_inc(task_dve, 1)
            dve.wait_ge(task_dve, 2)
            v.tensor_scalar(ts_[:, 1:2], ts_[:, 0:1], -1.0, None, ALU.mult).then_inc(task_dve, 1)
            dve.wait_ge(task_exp, 1)
            v.reciprocal(ts_[:, 3:4], ts_[:, 2:3]).then_inc(task_dve, 1)
            dve.wait_ge(task_dve, 4)
            v.tensor_scalar(tl[:, 2, :], tl[:, 1, :], ts_[:, 3:4], 0.5, ALU.mult, ALU.mult).then_inc(task_dve, 1)
            dve.wait_ge(td_ps, 1)
            v.tensor_copy(tdT[:, :], pb[5][0:ND, 32:32 + B]).then_inc(tdT_ok, 1)

            dve.wait_ge(ld_rb, 16)
            for half in range(2):
                own = slice(4 * half, 4 * half + 4)
                dve.wait_ge(logit_ps, half + 1)
                v.tensor_tensor(lb[:, own, 0:E], pb[LG_BANK[half]][:, 0:4 * E].rearrange("p (i e) -> p i e", e=E),
                                rb_sb[:, :].unsqueeze(1).broadcast_to([P, 4, E]), ALU.add).then_inc(lb_ok, 1)
                dve.wait_ge(lb_ok, half + 2)
                for i in range(4 * half, 4 * half + 4):
                    v.max(top8[:, i, :], lb[:, i, :]).then_inc(top_ok, 1)
            for half in range(2):
                dve.wait_ge(top_ok, 4 * half + 4)
                v.memset(top8[:, 4 * half:4 * half + 4, K:8], SENTINEL).then_inc(cut_ok, 1)
            for half in range(2):
                dve.wait_ge(cut_ok, half + 1)
                for i in range(4 * half, 4 * half + 4):
                    v.match_replace(marked[:, i, :], top8[:, i, :], lb[:, i, :], CHOSEN).then_inc(marked_ok, 1)
            for half in range(2):
                own = slice(4 * half, 4 * half + 4)
                dve.wait_ge(marked_ok, 4 * half + 4)
                v.tensor_scalar(chosen[:, own, :], marked[:, own, 0:E], CHOSEN, None, ALU.is_ge).then_inc(chosen_ok, 1)

            dve.wait_ge(logit_sb, 2)
            v.tensor_reduce(lmax[:, :], logit[:, :, :], AX.X, ALU.max).then_inc(lmax_ok, 1)
            dve.wait_ge(count_ps, 1)
            v.tensor_scalar(need[:, 0, :], pb[6][0:E, 0:P], 1.0 / P, 0.5 - 0.5 / P, ALU.mult, ALU.add).then_inc(need_ok, 1)
            dve.wait_ge(need_ok, 1)
            v.tensor_scalar(need_bf[:, :], need[:, 0, :], ROUND, -ROUND, ALU.add, ALU.add).then_inc(need_ok, 1)
            dve.wait_ge(rank_ps, 1)
            v.tensor_tensor(slotmap[:, :, :], pb[7][:, :].rearrange("p (i e) -> p i e", e=E), chosen[:, :, :], ALU.mult).then_inc(slot_ok, 1)
            dve.wait_ge(slot_ok, 1)
            for i in range(NT):
                v.max(slot8[:, i, :], slotmap[:, i, :]).then_inc(slot8_ok, 1)
            dve.wait_ge(slot8_ok, NT)
            v.tensor_scalar(slot_i[:, 0, :].rearrange("p (i k) -> p i k", k=K), slot8[:, :, 0:K], -1.0, None, ALU.add).then_inc(slotf, 1)
            dve.wait_ge(slotf, 1)
            v.tensor_scalar(slot_i[:, 1, :], slot_i[:, 0, :], P - 1, None, ALU.bitwise_and).then_inc(slotf, 1)
            v.tensor_scalar(slot_i[:, 2, :], slot_i[:, 0, :], 7, None, ALU.logical_shift_right).then_inc(slotf, 1)
            dve.wait_ge(slotf, 3)
            v.tensor_copy(slot_h[:, :, :], slot_i[:, 1:3, :]).then_inc(slotf, 1)
            dve.wait_ge(slotf, 4)
            for r in range(NJ // GJ):
                n, cols = r % 2, slice(r * GJ, (r + 1) * GJ)
                if r >= 2:
                    dve.wait_ge(listed, r - 1)
                    dve.wait_ge(valued, 2 * (r - 1))
                v.tensor_tensor(oh_tile[:, n, :, :], lanes[:, 0:MAXT, :],
                                slot_h[:, 1, cols].unsqueeze(1).broadcast_to([P, MAXT, GJ]), ALU.is_equal).then_inc(onehot, 1)
                v.tensor_tensor(oh_lane[:, n, :, :], lanes[:, :, :],
                                slot_h[:, 0, cols].unsqueeze(1).broadcast_to([P, P, GJ]), ALU.is_equal).then_inc(onehot, 1)
            dve.wait_ge(listed, NJ // GJ)
            v.tensor_scalar(empty[:, :], pb[6][:, 128:128 + MAXT], 0.0, SKIP, ALU.is_equal, ALU.mult).then_inc(tok_step, 1)
            dve.wait_ge(tok_step, 2)
            v.scalar_tensor_tensor(tok[:, 0:MAXT], pb[6][:, 128:128 + MAXT], -1.0, empty[:, :], ALU.add, ALU.add).then_inc(tok_step, 1)
            dve.wait_ge(tok_step, 3)
            for k in range(XB):
                v.tensor_copy(tok_now[:, k:k + 1], tok[:, k:k + 1]).then_inc(tok_set, 1)
            dve.wait_ge(rank_ps, 2)
            v.tensor_copy(cuml[:, :], pb[5][0:E, 128:129]).then_inc(cmp_ok, 1)
            v.tensor_scalar(turns_f[:, :], pb[5][0:1, 160:161], 1.0 / U, 0.5 - 0.5 / U, ALU.mult, ALU.add).then_inc(turns_step, 1)
            dve.wait_ge(turns_step, 1)
            v.tensor_scalar(turns[:, 0:1], turns_f[:, :], ROUND, -ROUND, ALU.add, ALU.add).then_inc(turns_step, 1)
            dve.wait_ge(turns_step, 2)
            v.tensor_scalar(turns[:, 1:2], turns[:, 0:1], -2.0, float(U), ALU.add, ALU.mult).then_inc(turns_step, 1)
            dve.wait_ge(cmp_ok, 1)
            v.tensor_scalar(cmp[:, :], lanes[0:E, 0:MAXT, 0], cuml[:, :], None, ALU.is_ge).then_inc(cmp_ok, 1)
            dve.wait_ge(expert_ps, 1)
            v.tensor_scalar(tile_e[:, 0, :], pb[5][:, 192:192 + MAXT], float(E - 1), None, ALU.min).then_inc(expert_step, 1)
            dve.wait_ge(expert_step, 1)
            dve.wait_ge(at_ok, 1)
            v.tensor_copy(gu_at[:, GU_LAG:GU_LAG + MAXT], tile_e[0:1, 0, :]).then_inc(at_ok, 1)
            v.tensor_scalar(tile_e[:, 1, :], tile_e[:, 0, :], 1, None, ALU.bitwise_and).then_inc(expert_step, 1)
            dve.wait_ge(expert_step, 2)
            v.tensor_copy(parity[:, 1, :], tile_e[:, 1, :]).then_inc(expert_step, 1)
            v.tensor_scalar(parity[:, 0, :], tile_e[:, 1, :], -1.0, 1.0, ALU.mult, ALU.add).then_inc(expert_step, 1)

            def weights_of_choices():
                dve.wait_ge(lexp_ok, 1)
                v.tensor_reduce(zden[:, 0, :], logit[:, :, :], AX.X, ALU.add).then_inc(w_step, 1)
                for j in range(NJ):
                    i, k = j // K, j % K
                    if j >= 4:
                        dve.wait_ge(pick_ok, j - 3)
                    v.scalar_tensor_tensor(junk[:, j % 4, :], slotmap[:, i, :], slot8[:, i, k:k + 1], logit[:, i, :],
                                           ALU.is_equal, ALU.mult, accum_out=pick[:, j:j + 1]).then_inc(pick_ok, 1)
                dve.wait_ge(pick_ok, NJ)
                pk = pick[:, :].rearrange("p (i k) -> p i k", k=K)
                v.tensor_reduce(zden[:, 1, :], pk, AX.X, ALU.add).then_inc(w_step, 1)
                dve.wait_ge(w_step, 2)
                v.scalar_tensor_tensor(zden[:, 2, :], zden[:, 0, :], 1e-8, zden[:, 1, :], ALU.mult, ALU.add).then_inc(w_step, 1)
                dve.wait_ge(w_step, 3)
                v.reciprocal(zden[:, 0, :], zden[:, 2, :]).then_inc(w_step, 1)
                dve.wait_ge(w_step, 4)
                v.tensor_tensor(wgt[:, :].rearrange("p (i k) -> p i k", k=K), pk,
                                zden[:, 0, :].unsqueeze(2).broadcast_to([P, NT, K]), ALU.mult).then_inc(w_step, 1)

            def unit(n):
                i, hc, blk = units[n]
                dve.wait_ge(unit_sb, 2 * n + 2 if n < EARLY else EARLY + n + 1)
                u = sgu_v[:, 1, n % 2, :] if n < EARLY else pb[2 * (n % 2) + 1][:, :]
                v.tensor_tensor(hsh[:, 2 * i + hc, blk * 512:(blk + 1) * 512], sgu_v[:, 0, n % 2, :], u,
                                ALU.mult).then_inc(unit_h, 1)

            counts = turn_count(dve), last_turn_end(dve)
            unit(0)
            dve.wait_ge(expert_step, 4)

            def stages(turn, first, k, have):
                if have(2):
                    q, n = first + (k - 2), (k - 2) % 2
                    dve.wait_ge(silu_ok, q + 1)
                    if have(4):
                        dve.wait_ge(hT_ps, q - 1)
                    for par in range(2):
                        ins = v.scalar_tensor_tensor(hh[:, n, par, :], sg[:, n, :], parity[:, par, bass.ds(q, 1)],
                                                     pb[2 + n][:, F:2 * F], ALU.mult, ALU.mult)
                    ins.then_inc(h_ok, 1)
                if have(0):
                    q, n = first + k, k % 2
                    dve.wait_ge(xT_ps, q + 1)
                    if have(2):
                        dve.wait_ge(gu_ps, q - 1)
                    v.tensor_copy(xgT[:, n, :, :], pb[n][:, 0:D].rearrange("p (c n) -> p c n", c=DC)).then_inc(xT_sb, 1)
                    v.tensor_copy(tok_now[:, k % XB:k % XB + 1], tok[:, bass.ds(q + XB, 1)]).then_inc(tok_set, 1)

            over_tiles(dve, stages, 3, counts)
            unit(1)
            weights_of_choices()

            def add_choice(j):
                i, k = j // K, j % K
                dve.wait_ge(back[j % NC], 16 * (j // NC + 1))
                if k:
                    dve.wait_ge(mixed, j)
                if j == NJ - 1:
                    dve.wait_ge(shared_in, NT)
                v.scalar_tensor_tensor(xs[:, i, :], z[:, j % NC, :], wgt[:, j:j + 1], xs[:, i, :],
                                       ALU.mult, ALU.add).then_inc(mixed, 1)

            def add_shared(i):
                dve.wait_ge(down_ps, i + 1)
                dve.wait_ge(mixed, min(K * (i + 1), NJ - 1))
                v.tensor_tensor(xs[:, i, :], pb[4 + i % 4][:, 0:D], xs[:, i, :], ALU.add).then_inc(shared_in, 1)

            unit(2)
            unit(3)
            dve.wait_ge(w_step, 5)
            for i in range(NT):
                for j in range(i * K, (i + 1) * K):
                    if j == NJ - 1:
                        add_shared(NT - 3)
                        add_shared(NT - 2)
                        add_shared(NT - 1)
                    add_choice(j)
                if i == 0:
                    unit(4)
                elif 2 <= i < NT - 1:
                    add_shared(i - 2)
                if 3 <= i < 6:
                    unit(2 + i)

        @block.tensor
        def _(pe):
            t = nc.tensor
            pe.wait_ge(ld_proj, 16)
            for blk in range(2):
                t.matmul(pb[blk][:, :], proj_sb[0:H, N:N + 2 * H], proj_sb[0:H, blk * 512:(blk + 1) * 512],
                         start=True, stop=True).then_inc(proj_ps, 1)
            for b in range(B):
                pe.wait_ge(qk_sb, 2 * (b // 2 + 1))
                for c in range(TPB):
                    q0 = b * S + c * P
                    ins = t.matmul(pb[4 + b][:, c * S:(c + 1) * S], qkT[0:H, 0, q0:q0 + P], qkT[0:H, 1, b * S:(b + 1) * S],
                                   start=True, stop=True)
                ins.then_inc(score_ps, 1)
            pe.wait_ge(const_ok, 9)

            def logits(b):
                pe.wait_ge(zT_sb, DC * (b + 1))
                if b == 0:
                    pe.wait_ge(ld_router, 16)
                if b % 2 == 0:
                    pe.wait_ge(score_x, LG_BANK[b // 2] - 3)
                for c in range(TPB):
                    i = TPB * b + c
                    for h in range(DC):
                        t.matmul(pb[LG_BANK[b // 2]][:, i % 4 * E:(i % 4 + 1) * E], zT[:, h, i * P:(i + 1) * P], wr_sb[:, h, :],
                                 start=(i % 4 == 0 and h == 0), stop=False, skip_group_check=True)

            def unit(n, g, halves=(0, 1)):
                i, hc, blk = units[n]
                if n == 0 and g == 0:
                    pe.wait_ge(ld_shared, 16)
                if 2 <= n < EARLY + 2:
                    pe.wait_ge(unit_sb, 2 * (n - 1))
                elif n >= EARLY + 2:
                    pe.wait_ge(unit_h, n - 1)
                for h in halves:
                    ins = t.matmul(pb[2 * (n % 2) + g][:, :], sgu_sb[:, i, g, h, hc * P:(hc + 1) * P],
                                   zT[:, h, blk * 512:(blk + 1) * 512], start=(h == 0), stop=(h == DC - 1),
                                   skip_group_check=True)
                if g and 1 in halves:
                    ins.then_inc(unit_ps, 1)

            for b in range(B):
                pe.wait_ge(z_ok, TPB * (b + 1))
                for h in range(DC):
                    for c in range(TPB):
                        i = TPB * b + c
                        ins = t.transpose(pb[b][:, h * S + c * P:h * S + (c + 1) * P], z[:, i, h::DC], ident[:, :])
                ins.then_inc(zT_ps, 1)
                if b >= 1:
                    logits(b - 1)
            pe.wait_ge(zT_sb, DC * B)
            pe.wait_ge(score_x, B)
            for h in range(DC):
                ins = t.matmul(pb[5][:, 0:B], te1_sb[:, h, :], zsum[:, h, :], start=(h == 0), stop=(h == DC - 1))
            ins.then_inc(h1_ps, 1)
            pe.wait_ge(h1_ok, 1)
            t.matmul(pb[5][0:B, 16:16 + ND], h1[:, :], te2_sb, start=True, stop=True).then_inc(tl_ps, 1)
            logits(B - 1)
            pe.wait_ge(task_dve, 5)
            t.transpose(pb[5][0:ND, 32:32 + B], tl[:, 2, :], ident[0:B, 0:B]).then_inc(td_ps, 1)
            pe.wait_ge(tdT_ok, 1)
            pe.wait_ge(ld_task, 16)
            for b in range(B):
                ins = t.matmul(pb[LG_BANK[b // 2]][:, b % 2 * TPB * E:(b % 2 + 1) * TPB * E].rearrange("p (i e) -> p i e", e=E),
                               tdT[:, b:b + 1].broadcast_to([ND, P]), aff_sb[:, :].unsqueeze(1).broadcast_to([ND, TPB, E]),
                               start=False, stop=(b % 2 == 1), skip_group_check=True)
                if b % 2:
                    ins.then_inc(logit_ps, 1)
            unit(0, 0)
            pe.wait_ge(logit_sb, 2)
            for i in range(NT):
                if i % 4 == 0:
                    pe.wait_ge(chosen_ok, i // 4 + 1)
                ins = t.matmul(pb[6][0:E, 0:P], chosen[:, i, :], ones_bf[:, :], start=(i == 0), stop=(i == NT - 1))
            ins.then_inc(count_ps, 1)
            t.matmul(pb[7][:, :], tri[:, :], chosen[:, :, :].rearrange("p i e -> p (i e)"), start=True, stop=False, skip_group_check=True)
            for i in range(NT - 1):
                t.matmul(pb[7][:, (i + 1) * E:].rearrange("p (i e) -> p i e", e=E), ones_bf[:, :],
                         chosen[:, i, :].unsqueeze(1).broadcast_to([P, NT - 1 - i, E]),
                         start=False, stop=False, skip_group_check=True)
            pe.wait_ge(need_ok, 2)
            t.matmul(pb[7][:, :].rearrange("p (i e) -> p i e", e=E), need_bf[:, :],
                     tri_less[:, :].unsqueeze(1).broadcast_to([E, NT, E]),
                     start=False, stop=True, skip_group_check=True).then_inc(rank_ps, 1)
            t.matmul(pb[5][0:E, 128:129], tri[0:E, 0:E], need_bf[:, 0:1], start=True, stop=True)
            t.matmul(pb[5][0:1, 160:161], need_bf[:, 0:1], ones_bf[0:E, 0:1], start=True, stop=True).then_inc(rank_ps, 1)
            unit(0, 1)
            unit(1, 0)
            for r in range(NJ // GJ):
                pe.wait_ge(onehot, 2 * (r + 1))
                pe.wait_ge(valued, 2 * (r + 1))
                for j in range(GJ):
                    ins = t.matmul(pb[6][:, 128:128 + MAXT], oh_lane[:, r % 2, :, j], oh_val[:, r % 2, :, j],
                                   start=(r == 0 and j == 0), stop=(r == NJ // GJ - 1 and j == GJ - 1))
                ins.then_inc(listed, 1)
            pe.wait_ge(cmp_ok, 2)
            t.matmul(pb[5][:, 192:192 + MAXT], ones_bf[0:E, :], cmp[:, :], start=True, stop=True).then_inc(expert_ps, 1)
            unit(1, 1)

            pe.wait_ge(unit_sb, 2)
            for n in range(8):
                pe.wait_ge(ld_gu[n], 16)
            for n in range(4):
                pe.wait_ge(ld_d[n], 16)

            def stages(turn, first, k, have):
                if have(0):
                    q = first + k
                    pe.wait_ge(got[k % XB], (turn * (U // XB) + (k // XB + 1)) * 16)
                    if have(2):
                        pe.wait_ge(xT_sb, q - 1)
                    for h in range(DC):
                        ins = t.transpose(pb[k % 2][:, h * P:(h + 1) * P], xg[:, k % XB, h::DC], ident[:, :])
                    ins.then_inc(xT_ps, 1)
                if k < 4 and have(U):
                    gu_of[k] = pe.snap(next_gu[k], min_val=0, max_val=E - 1)
                elif k % 4 == 0:
                    gu_of[k:k + 4] = load_at(first + k)
                if have(1):
                    q, n = first + (k - 1), (k - 1) % 2
                    pe.wait_ge(xT_sb, q + 1)
                    if not have(2):
                        pe.wait_ge(unit_sb, 2 * EARLY)
                    if have(3):
                        pe.wait_ge(h_ok, q - 1)
                    for h in range(DC):
                        ins = t.matmul(pb[2 + n][:, 0:2 * F], xgT[:, n, h, :],
                                       wgu_sb[:, bass.ds(gu_of[k], 1), h, :].rearrange("p o f -> p (o f)"),
                                       start=(h == 0), stop=(h == DC - 1))
                    ins.then_inc(gu_ps, 1)
                if k == U - 3:
                    for reg, e in zip(next_gu, load_at(first + U)):
                        pe.reg_mov(reg, e)
                if k == U - 1:
                    for reg, e in zip(last_gu, gu_of[U - (D_LAG - GU_LAG):]):
                        pe.reg_mov(reg, e)
                if k < D_LAG - GU_LAG:
                    if have(U):
                        d_of[k] = pe.snap(last_gu[k], min_val=0, max_val=E - 1) // 2
                else:
                    d_of[k] = gu_of[k - (D_LAG - GU_LAG)] // 2
                if have(3):
                    q, n = first + (k - 3), (k - 3) % 2
                    pe.wait_ge(h_ok, q + 1)
                    if have(4):
                        pe.wait_ge(hT_sb, q)
                    t.transpose(pb[6][:, 0:P], hh[:, n, :, :].rearrange("p a f -> p (a f)"), ident[:, :]).then_inc(hT_ps, 1)
                if have(4):
                    q, n = first + (k - 4), (k - 4) % 2
                    pe.wait_ge(hT_sb, q + 1)
                    if have(6):
                        pe.wait_ge(y_sb, q - 1)
                    t.matmul(pb[4 + n][:, 0:D], hT[:, n, :],
                             wd_sb[:, bass.ds(d_of[k], 1), :].rearrange("p o d -> p (o d)"),
                             start=True, stop=True).then_inc(y_ps, 1)

            gu_of, d_of = [None] * U, [None] * U

            last_gu = [ctx.enter_context(pe.register(f"last_gu{n}")) for n in range(D_LAG - GU_LAG)]
            next_gu = [ctx.enter_context(pe.register(f"next_gu{n}")) for n in range(4)]

            def load_at(step):
                _, vals = nc.values_load_multi_w_load_instructions(
                    gu_at[0:1, bass.ds(step, 4)], engines=[mybir.EngineType.PE], min_val=0, max_val=E - 1,
                    skip_runtime_bounds_check_because="VectorE has bounded the expert of every tile by E - 1")
                return list(vals)

            pe.wait_ge(at_ok, 2)
            end = over_tiles(pe, stages, 5)
            pe.wait_ge(xT_sb, end)
            pe.wait_ge(h_ok, end)
            pe.wait_ge(y_sb, end)

            def shared_out(i):
                if i >= 4:
                    pe.wait_ge(shared_in, i - 3)
                for q in range(NSH * DC):
                    ins = t.matmul(pb[4 + i % 4][:, 0:D], hsh[:, q, i * P:(i + 1) * P], sd_sb[:, q, :],
                                   start=(q == 0), stop=(q == NSH * DC - 1))
                ins.then_inc(down_ps, 1)

            for blk in range(2):
                for n in range(*((EARLY, 5), (5, len(units)))[blk]):
                    unit(n, 0)
                    unit(n, 1)
                pe.wait_ge(unit_h, (5, len(units))[blk])
                for i in range(blk * NT // 2, (blk + 1) * NT // 2):
                    shared_out(i)


def kernel(x, ctx_512, mask_SxS2_bk1, mask_BxS2_bf0, L0_xattn_Wq, L0_xattn_bq, L0_xattn_Wk, L0_xattn_bk,
           L0_ffn_Wr, L0_ffn_router_bias, L0_ffn_affinity, L0_ffn_te_W1, L0_ffn_te_b1, L0_ffn_te_W2,
           L0_ffn_te_b2, L0_ffn_Wg, L0_ffn_Wu, L0_ffn_Wd, L0_ffn_Sg, L0_ffn_Su, L0_ffn_Sd):
    import numpy as np
    import concourse.bacc as bacc
    from concourse.bass_utils import run_bass_kernel_spmd

    def by_feature(w):
        return w.reshape(P, DC, -1)

    sgu = np.stack([np.stack([by_feature(L0_ffn_Sg[i]), by_feature(L0_ffn_Su[i])], 1) for i in range(NSH)], 1)
    sd = L0_ffn_Sd.reshape(NSH * DC, P, D).transpose(1, 0, 2)
    arrays = {
        "x": x.reshape(N, D),
        "proj": np.concatenate([ctx_512.reshape(N, H).T, L0_xattn_Wq.T, L0_xattn_Wk.T,
                                L0_xattn_bq[:, None], L0_xattn_bk[:, None]], 1),
        "amask": mask_SxS2_bk1,
        "kmask": mask_BxS2_bf0.reshape(B * S),
        "router": np.concatenate([by_feature(L0_ffn_Wr.T).reshape(P, -1), by_feature(L0_ffn_te_W1.T).reshape(P, -1),
                                  L0_ffn_te_W2.T, L0_ffn_te_b1[:, None]], 1),
        "task": L0_ffn_affinity.T,
        "b2": L0_ffn_te_b2,
        "rbias": L0_ffn_router_bias,
        "shared": np.concatenate([sgu.reshape(P, -1), sd.reshape(P, -1)], 1),
        "wgu": np.stack([L0_ffn_Wg.reshape(E, P, DC, F), L0_ffn_Wu.reshape(E, P, DC, F)], 3).reshape(E, P, -1),
        "wd": L0_ffn_Wd,
    }
    arrays = {k: np.ascontiguousarray(v) for k, v in arrays.items()}
    nc = bacc.Bacc("TRN2", target_bir_lowering=False, num_devices=1)
    aps = {k: nc.dram_tensor(f"in_{k}", v.shape, mybir.dt.from_np(v.dtype), kind="ExternalInput").ap() for k, v in arrays.items()}
    out = nc.dram_tensor("out", (N, D), F32, kind="ExternalOutput").ap()
    build_xattn_moe(nc, *aps.values(), out)
    r = run_bass_kernel_spmd(nc, [{f"in_{k}": v for k, v in arrays.items()}], core_ids=[0])
    return r.results[0]["out"].reshape(B, S, D)
```
